# Optimizing a Trainium2 kernel written in Bass

```python
import numpy as np
import jax
import jax.numpy as jnp

def _softmax(x, axis=-1):
    return jax.nn.softmax(x, axis=axis)

def _gelu(x):
    return jax.nn.gelu(x, approximate=True)

def _silu(x):
    return jax.nn.silu(x)

def _sigmoid(x):
    return jax.nn.sigmoid(x)

def _layernorm(x, axis=-1, eps=1e-05):
    m = jnp.mean(x, axis=axis, keepdims=True)
    v = jnp.var(x, axis=axis, keepdims=True)
    return (x - m) / jnp.sqrt(v + eps)

def _scatter_add(tgt, idx, src, axis=0):
    return tgt.at[idx].add(src)

def _segment_sum(src, seg, n):
    return jax.ops.segment_sum(src, seg, n)
kernel_name = 'mk_lm_tower_d1_tok_ids256_r4_10e1e6'

def setup_inputs(seed: int=0):
    np.random.seed(seed)
    _w = jnp.asarray

    def _rec_inputs():
        import jax
        import jax.numpy as jnp
        _rk = jax.random.key(seed)
        x = jax.random.randint(jax.random.fold_in(_rk, 1), (16, 512), 0, 7, jnp.int32)
        itok_BS_0_23 = jax.random.randint(jax.random.fold_in(_rk, 21), (16, 512), 0, 24, jnp.int32)
        itok_BS_0_11 = jax.random.randint(jax.random.fold_in(_rk, 22), (16, 512), 0, 12, jnp.int32)
        itok_BS_0_30 = jax.random.randint(jax.random.fold_in(_rk, 23), (16, 512), 0, 31, jnp.int32)
        return (x, itok_BS_0_23, itok_BS_0_11, itok_BS_0_30)
    x, itok_BS_0_23, itok_BS_0_11, itok_BS_0_30 = _rec_inputs()

    def _L0_tok_setup():
        import jax, jax.numpy as jnp
        import numpy as np
        import math
        B, S = (64, 512)
        HARM = 3
        N_PERIODS = 4
        FD = N_PERIODS * 2 * HARM
        TD = 64
        PERIODS = np.array([7.0, 24.0, 12.0, 1.0], dtype=np.float32)
        LN_EPS = 1e-05

        def _fourier_concat(dayofweek, hour, month, dayofmonth, hw, ph):
            t = jnp.stack([dayofweek, hour, month, dayofmonth]).astype(jnp.float32)
            periods = jnp.asarray(PERIODS)
            norm = 2.0 * math.pi * t / periods[:, None, None]
            h = jnp.arange(1, HARM + 1, dtype=jnp.float32)
            ang = norm[..., None] * h + ph[:, None, None, :]
            w = hw[:, None, None, :]
            f = jnp.stack([w * jnp.sin(ang), w * jnp.cos(ang)], axis=-1)
            return jnp.moveaxis(f, 0, 2).reshape(t.shape[1], t.shape[2], FD)
        key = jax.random.key(seed)
        ks = jax.random.split(key, 12)
        maxv = [7, 24, 12, 31]
        times = {n: jax.random.randint(ks[i], (B, S), 0, maxv[i], dtype=jnp.int32) for i, n in enumerate(['dayofweek', 'hour', 'month', 'dayofmonth'])}
        inp = dict(times)
        inp['hw'] = jax.random.uniform(ks[4], (N_PERIODS, HARM), dtype=jnp.float32) + 0.5
        inp['ph'] = jax.random.normal(ks[5], (N_PERIODS, HARM), dtype=jnp.float32) * 0.1
        inp['W1'] = jax.random.normal(ks[6], (FD, 2 * TD), dtype=jnp.float32) / math.sqrt(FD)
        inp['b1'] = jax.random.normal(ks[7], (2 * TD,), dtype=jnp.float32) * 0.01
        inp['W2'] = jax.random.normal(ks[8], (2 * TD, TD), dtype=jnp.float32) / math.sqrt(2 * TD)
        inp['b2'] = jax.random.normal(ks[9], (TD,), dtype=jnp.float32) * 0.01
        inp['gamma'] = jnp.ones((TD,), dtype=jnp.float32)
        inp['beta'] = jnp.zeros((TD,), dtype=jnp.float32)
        inp['Wres'] = jax.random.normal(ks[10], (FD, TD), dtype=jnp.float32) / math.sqrt(FD)
        inp['bres'] = jax.random.normal(ks[11], (TD,), dtype=jnp.float32) * 0.01
        return inp
    _L0_tok_all = _L0_tok_setup()
    _L0_tok_in = {k: v for k, v in _L0_tok_all.items() if k in ('hw', 'ph', 'W1', 'b1', 'W2', 'b2', 'gamma', 'beta', 'Wres', 'bres')}
    del _L0_tok_all

    def _L0_attn_setup():
        import jax, jax.numpy as jnp
        import numpy as np
        B, S, C = (8, 256, 64)
        H, KD = (8, 64)
        HEAD_DIM = KD // H
        key = jax.random.key(seed)
        ks = jax.random.split(key, 5)
        sc = 0.02
        return {'x': jax.random.normal(ks[0], (B, S, C), dtype=jnp.float32), 'Wq': jax.random.normal(ks[1], (H * KD, C), dtype=jnp.float32) * sc, 'Wk': jax.random.normal(ks[2], (KD, C), dtype=jnp.float32) * sc, 'Wv': jax.random.normal(ks[3], (KD, C), dtype=jnp.float32) * sc, 'Wo': jax.random.normal(ks[4], (C, H * KD), dtype=jnp.float32) * sc}
    _L0_attn_all = _L0_attn_setup()
    _L0_attn_in = {k: v for k, v in _L0_attn_all.items() if k in ('Wq', 'Wk', 'Wv', 'Wo')}
    del _L0_attn_all

    def _L0_ffn_setup():
        import jax, jax.numpy as jnp
        import numpy as np
        E, D, H, TOP_K = (6, 64, 64, 2)
        ROUTER_H = D // 2
        key = jax.random.key(seed)
        ks = jax.random.split(key, 12)
        s = 1.0 / np.sqrt(D)
        sh = 1.0 / np.sqrt(H)
        sr = 1.0 / np.sqrt(ROUTER_H)
        return {'features': jax.random.normal(ks[0], (8, 1024, D), dtype=jnp.float32), 'router_w1': jax.random.uniform(ks[1], (D, ROUTER_H), jnp.float32, -s, s), 'router_b1': jnp.zeros((ROUTER_H,), jnp.float32), 'router_w2': jax.random.uniform(ks[2], (ROUTER_H, E), jnp.float32, -sr, sr), 'router_b2': jnp.zeros((E,), jnp.float32), 'expert_w1': jax.random.uniform(ks[3], (E, D, H), jnp.float32, -s, s), 'expert_b1': jnp.zeros((E, H), jnp.float32), 'expert_w2': jax.random.uniform(ks[4], (E, H, H), jnp.float32, -sh, sh), 'expert_b2': jnp.zeros((E, H), jnp.float32), 'expert_w3': jax.random.uniform(ks[5], (E, H, D), jnp.float32, -sh, sh), 'expert_b3': jnp.zeros((E, D), jnp.float32)}
    _L0_ffn_all = _L0_ffn_setup()
    _L0_ffn_in = {k: v for k, v in _L0_ffn_all.items() if k in ('router_w1', 'router_b1', 'router_w2', 'router_b2', 'expert_w1', 'expert_b1', 'expert_w2', 'expert_b2', 'expert_w3', 'expert_b3')}
    del _L0_ffn_all
    return {'x': x, 'itok_BS_0_23': itok_BS_0_23, 'itok_BS_0_11': itok_BS_0_11, 'itok_BS_0_30': itok_BS_0_30, 'L0_tok_hw': _L0_tok_in['hw'], 'L0_tok_ph': _L0_tok_in['ph'], 'L0_tok_W1': _L0_tok_in['W1'], 'L0_tok_b1': _L0_tok_in['b1'], 'L0_tok_W2': _L0_tok_in['W2'], 'L0_tok_b2': _L0_tok_in['b2'], 'L0_tok_gamma': _L0_tok_in['gamma'], 'L0_tok_beta': _L0_tok_in['beta'], 'L0_tok_Wres': _L0_tok_in['Wres'], 'L0_tok_bres': _L0_tok_in['bres'], 'L0_attn_Wq': _L0_attn_in['Wq'], 'L0_attn_Wk': _L0_attn_in['Wk'], 'L0_attn_Wv': _L0_attn_in['Wv'], 'L0_attn_Wo': _L0_attn_in['Wo'], 'L0_ffn_router_w1': _L0_ffn_in['router_w1'], 'L0_ffn_router_b1': _L0_ffn_in['router_b1'], 'L0_ffn_router_w2': _L0_ffn_in['router_w2'], 'L0_ffn_router_b2': _L0_ffn_in['router_b2'], 'L0_ffn_expert_w1': _L0_ffn_in['expert_w1'], 'L0_ffn_expert_b1': _L0_ffn_in['expert_b1'], 'L0_ffn_expert_w2': _L0_ffn_in['expert_w2'], 'L0_ffn_expert_b2': _L0_ffn_in['expert_b2'], 'L0_ffn_expert_w3': _L0_ffn_in['expert_w3'], 'L0_ffn_expert_b3': _L0_ffn_in['expert_b3']}

def reference(x, itok_BS_0_23, itok_BS_0_11, itok_BS_0_30, L0_tok_hw, L0_tok_ph, L0_tok_W1, L0_tok_b1, L0_tok_W2, L0_tok_b2, L0_tok_gamma, L0_tok_beta, L0_tok_Wres, L0_tok_bres, L0_attn_Wq, L0_attn_Wk, L0_attn_Wv, L0_attn_Wo, L0_ffn_router_w1, L0_ffn_router_b1, L0_ffn_router_w2, L0_ffn_router_b2, L0_ffn_expert_w1, L0_ffn_expert_b1, L0_ffn_expert_w2, L0_ffn_expert_b2, L0_ffn_expert_w3, L0_ffn_expert_b3):
    import jax
    import jax.numpy as jnp

    def _L0_tok_ref(dayofweek, hour, month, dayofmonth, hw, ph, W1, b1, W2, b2, gamma, beta, Wres, bres):
        import jax, jax.numpy as jnp
        import numpy as np
        import math
        B, S = (64, 512)
        HARM = 3
        N_PERIODS = 4
        FD = N_PERIODS * 2 * HARM
        TD = 64
        PERIODS = np.array([7.0, 24.0, 12.0, 1.0], dtype=np.float32)
        LN_EPS = 1e-05

        def _fourier_concat(dayofweek, hour, month, dayofmonth, hw, ph):
            t = jnp.stack([dayofweek, hour, month, dayofmonth]).astype(jnp.float32)
            periods = jnp.asarray(PERIODS)
            norm = 2.0 * math.pi * t / periods[:, None, None]
            h = jnp.arange(1, HARM + 1, dtype=jnp.float32)
            ang = norm[..., None] * h + ph[:, None, None, :]
            w = hw[:, None, None, :]
            f = jnp.stack([w * jnp.sin(ang), w * jnp.cos(ang)], axis=-1)
            return jnp.moveaxis(f, 0, 2).reshape(t.shape[1], t.shape[2], FD)
        x = _fourier_concat(dayofweek, hour, month, dayofmonth, hw, ph)
        h1 = jax.nn.relu(jnp.einsum('bsf,fd->bsd', x, W1) + b1)
        h2 = jnp.einsum('bsd,dt->bst', h1, W2) + b2
        mu = jnp.mean(h2, axis=-1, keepdims=True)
        var = jnp.mean(jnp.square(h2 - mu), axis=-1, keepdims=True)
        ln = (h2 - mu) * jax.lax.rsqrt(var + LN_EPS) * gamma + beta
        residual = jnp.einsum('bsf,ft->bst', x, Wres) + bres
        return ln + 0.1 * residual

    def _L0_attn_ref(x, Wq, Wk, Wv, Wo):
        import jax, jax.numpy as jnp
        import numpy as np
        B, S, C = (8, 256, 64)
        H, KD = (8, 64)
        HEAD_DIM = KD // H
        b, s, c = x.shape
        q = jnp.einsum('bsc,oc->bso', x, Wq).reshape(b, s, H, KD).transpose(0, 2, 1, 3)
        k = jnp.einsum('bsc,oc->bos', x, Wk)
        v_conv = jnp.einsum('bsc,oc->bos', x, Wv)
        v = v_conv.reshape(b, s, KD)
        scale = 1.0 / np.sqrt(HEAD_DIM).astype(np.float32)
        scores = jnp.einsum('bhsd,bdt->bhst', q, k) * scale
        attn = jax.nn.softmax(scores, axis=-1)
        ctx = jnp.einsum('bhst,btd->bhsd', attn, v)
        ctx = ctx.transpose(0, 2, 1, 3).reshape(b, H * KD, s)
        out = jnp.einsum('bcp,oc->bop', ctx, Wo)
        return out.transpose(0, 2, 1)

    def _L0_ffn_ref(features, router_w1, router_b1, router_w2, router_b2, expert_w1, expert_b1, expert_w2, expert_b2, expert_w3, expert_b3):
        import jax, jax.numpy as jnp
        import numpy as np
        E, D, H, TOP_K = (6, 64, 64, 2)
        ROUTER_H = D // 2
        rh = jax.nn.relu(features @ router_w1 + router_b1)
        expert_logits = jax.nn.softmax(rh @ router_w2 + router_b2, axis=-1)
        top_w, top_i = jax.lax.top_k(expert_logits, TOP_K)
        routing_weights = jax.nn.softmax(top_w, axis=-1)
        h1 = jax.nn.relu(jnp.einsum('bsd,edh->bseh', features, expert_w1) + expert_b1)
        h2 = jax.nn.relu(jnp.einsum('bseh,ehf->bsef', h1, expert_w2) + expert_b2)
        expert_out = jnp.einsum('bsef,efo->bseo', h2, expert_w3) + expert_b3
        sel = jnp.take_along_axis(expert_out, top_i[:, :, :, None], axis=2)
        combined = jnp.sum(sel * routing_weights[..., None], axis=2)
        return combined
    h = _L0_tok_ref(x, itok_BS_0_23, itok_BS_0_11, itok_BS_0_30, L0_tok_hw, L0_tok_ph, L0_tok_W1, L0_tok_b1, L0_tok_W2, L0_tok_b2, L0_tok_gamma, L0_tok_beta, L0_tok_Wres, L0_tok_bres)
    h = h + _L0_attn_ref(_layernorm(h, axis=-1), L0_attn_Wq, L0_attn_Wk, L0_attn_Wv, L0_attn_Wo)
    h = h + _L0_ffn_ref(_layernorm(h, axis=-1), L0_ffn_router_w1, L0_ffn_router_b1, L0_ffn_router_w2, L0_ffn_router_b2, L0_ffn_expert_w1, L0_ffn_expert_b1, L0_ffn_expert_w2, L0_ffn_expert_b2, L0_ffn_expert_w3, L0_ffn_expert_b3)
    return h

_drawn_inputs = setup_inputs


def setup_inputs(seed=0):
    import zlib

    import numpy as np

    out = dict(_drawn_inputs(seed))
    spreads = {'L0_tok_gamma': (1.0, 0.2),
     'L0_tok_beta': (0.0, 0.1),
     'L0_ffn_router_b1': (0.0, 0.1),
     'L0_ffn_router_b2': (0.0, 0.1),
     'L0_ffn_expert_b1': (0.0, 0.743),
     'L0_ffn_expert_b2': (0.0, 0.275),
     'L0_ffn_expert_b3': (0.0, 0.1)}
    factors = {'L0_tok_b1': 3.251,
     'L0_tok_bres': 28.348,
     'L0_attn_Wq': 8.0,
     'L0_attn_Wk': 8.0,
     'L0_attn_Wv': 8.0,
     'L0_attn_Wo': 8.0}
    for name, (base, spread) in spreads.items():
        noise = np.random.default_rng([zlib.crc32(name.encode()), seed]).standard_normal(out[name].shape)
        drawn = base * np.exp(spread * noise) if base else spread * noise
        out[name] = jnp.asarray(drawn.astype(out[name].dtype))
    for name, factor in factors.items():
        out[name] = (out[name] * factor).astype(out[name].dtype)
    return out
```

```python
import math
from contextlib import ExitStack

import numpy as np
import concourse.bass as bass
from concourse import mybir

B, S, C = 16, 512, 64
HEADS, KD = 8, 64
NE = 6
EP = NE // 2
HARM, PERIODS = 3, (7.0, 24.0, 12.0, 1.0)
FD = 2 * HARM * len(PERIODS)
FR = FD + 1
PAIRS = B // 2
TOK = 2 * S
HP = 2 * HEADS
SLOTS = 4 * HP
LAG = 7
GROUPS = 4
GCOL = B * S // GROUPS
LN_EPS = 1e-5
SCORE_SCALE = float(np.float32(1.0) / np.sqrt(KD // HEADS).astype(np.float32))

LAYOUT, WIDTH = {}, 0
for _name, _w in (("wv", 128), ("rw1", 128), ("e1", EP * 128), ("fourier", 7), ("wq", HEADS * 128),
                  ("wk", 128), ("wo", 4 * C), ("w1", 128), ("wres", 128), ("w2", C), ("gamma", C),
                  ("beta", C), ("rw2", NE), ("rb1", 1), ("e1b", EP), ("e2", EP * 128), ("e2b", EP),
                  ("e3", EP * 128), ("e3b", NE * C), ("ident", 128), ("rank", NE)):
    LAYOUT[_name] = (WIDTH, WIDTH + _w)
    WIDTH += _w
SPLIT = LAYOUT["e1"][1]
EARLY = LAYOUT["wq"][0]

P_H1, P_TOK, P_LNA, P_LNA2, P_LNB, P_LNB2 = (0, 2), (4, 6), 7, 10, 14, 17
P_T, P_V = (21, 23), (25, 27)
F_FIN, F_LN, F_LN2, F_T, F_R, F_L = 9, 10, 14, (18, 20), (22, 24), 26
F_GATE = 29
F_H1 = {(0, 0): 28, (0, 1): 30, (0, 2): 32, (1, 0): 40, (1, 1): 42, (1, 2): 44}
F_H2 = {(0, 0): 34, (0, 1): 36, (0, 2): 38, (1, 0): 46, (1, 1): 48, (1, 2): 50}
F_Y = (40, 42, 44, 46, 52, 54, 56, 58)


def tower(nc, ids, consts, out):
    F32, F32R, I32 = mybir.dt.float32, mybir.dt.float32r, mybir.dt.int32
    ALU, ACT, AX = mybir.AluOpType, mybir.ActivationFunctionType, mybir.AxisListType

    feat_dram = nc.dram_tensor("feat_scratch", (GROUPS, FR, GCOL), F32, kind="Internal").ap()

    ctx = ExitStack()
    with ctx:
        def sb(name, shape, dt=F32):
            return ctx.enter_context(nc.sbuf_tensor(name, shape, dt))

        def pb(name):
            return ctx.enter_context(nc.psum_tensor(name, [128, 512], F32))

        def sem(name):
            return ctx.enter_context(nc.semaphore(name))

        cst = sb("cst", [128, WIDTH])

        def k(name):
            return cst[:, LAYOUT[name][0]:LAYOUT[name][1]]

        wsp = sb("wsp", [128, SPLIT], F32R)
        qk = sb("qk", [128, HEADS, 128], F32R)
        ids_sb = sb("ids_sb", [128, GCOL], I32)
        ang = sb("ang", [128, GCOL])
        turns = sb("turns", [128, GCOL])
        per_turn = sb("per_turn", [128, 1])
        power = sb("power", [128, 8])
        feat = sb("feat", [128, TOK])
        h1t = sb("h1t", [128, TOK])
        tok = sb("tok", [128, 8, 128])
        xc = [sb(f"xc{n}", [128, 8, C]) for n in range(3)]
        sq = [sb(f"sq{n}", [128, 8, C]) for n in range(3)]
        st = [sb(f"st{n}", [128, 5, 8]) for n in range(3)]
        h = sb("h", [128, 2, 8, C])
        xn = sb("xn", [128, 8, 2, C])
        kh = sb("kh", [128, 2, 2, S], F32R)
        kl = sb("kl", [128, 2, 2, S], F32R)
        v = sb("v", [128, 2, 2, 4, C])
        g = sb("g", [128, 2, S], F32R)
        p = sb("p", [128, 8, S])
        nmax = sb("nmax", [128, 8])
        z = sb("z", [128, 8])
        rz = sb("rz", [128, 8])
        woz = sb("woz", [128, 2, 4, C])
        m = sb("m", [128, 2, 2, 4, HEADS, C])
        hatt = sb("hatt", [128, 8, C])
        x2 = sb("x2", [128, 8, 2, C])
        xh = sb("xh", [128, TOK], F32R)
        xl = sb("xl", [128, TOK], F32R)
        rh = sb("rh", [128, TOK])
        gt = sb("gt", [128, 9, 8, NE])
        gs = sb("gs", [128, 10, 8])
        e1t = sb("e1t", [128, EP, S])
        e2t = sb("e2t", [128, EP, TOK])
        y = sb("y", [128, 2, NE, C])
        ys = sb("ys", [128, 2, 4, C])
        o = sb("o", [128, 8, C])

        s_bank = [pb(f"s_bank{n}") for n in range(4)]
        m_bank, g_bank, r_bank, f_bank = pb("m_bank"), pb("g_bank"), pb("r_bank"), pb("f_bank")

        (load_ids, load_cst, load_cst2, stored, feat_in, feat_zero) = [
            sem(x) for x in ("load_ids", "load_cst", "load_cst2", "stored", "feat_in", "feat_zero")]
        (inverse, power_set, angle, sine, feats, wsplit, qk_ps, qk_hi, qk_lo) = [
            sem(x) for x in ("inverse", "power_set", "angle", "sine", "feats", "wsplit", "qk_ps", "qk_hi", "qk_lo")]
        (score, maxed, expd, rzd, wozd, pvd, mevd, gps, ghi, glo) = [
            sem(x) for x in ("score", "maxed", "expd", "rzd", "wozd", "pvd", "mevd", "gps", "ghi", "glo")]
        (h1_ps, h1_sb, tok_ps, tok_sb, h_sb, t_ps, kh_sb, kl_sb, v_ps, v_sb) = [
            sem(x) for x in ("h1_ps", "h1_sb", "tok_ps", "tok_sb", "h_sb", "t_ps", "kh_sb", "kl_sb", "v_ps", "v_sb")]
        ln_dve = [sem(f"ln_dve{n}") for n in range(3)]
        ln_pool = [sem(f"ln_pool{n}") for n in range(3)]
        (fin_ps, hatt_sb, x2t_ps, xh_sb, xl_sb, rh_ps, rh_sb, l_ps, gate, gate_act) = [
            sem(x) for x in ("fin_ps", "hatt_sb", "x2t_ps", "xh_sb", "xl_sb", "rh_ps", "rh_sb", "l_ps", "gate", "gate_act")]
        (e1_ps, e1_sb, e2_ps, e2_sb, y_ps, y_sb, y_pool, gated) = [
            sem(x) for x in ("e1_ps", "e1_sb", "e2_ps", "e2_sb", "y_ps", "y_sb", "y_pool", "gated")]

        LN_DVE, LN_POOL = 4, (6, 5, 5)
        GATE = 22

        def wait(eng, s, value):
            if isinstance(value, int) and value <= 0:
                return
            eng.wait_ge(s, value)

        block = ctx.enter_context(nc.Block())

        @block.sync
        def _(sp):
            sp.dma_start(ids_sb[:, :], ids).then_inc(load_ids, 16)
            sp.dma_start(cst[:, 0:EARLY], consts[:, 0:EARLY]).then_inc(load_cst, 16)
            sp.dma_start(cst[:, EARLY:], consts[:, EARLY:]).then_inc(load_cst2, 16)
            sp.wait_ge(feats, 1)
            for q in range(GROUPS):
                sp.dma_start(feat_dram[q, :, :], ang[32 * q:32 * q + FR, :]).then_inc(stored, 16)
            sp.wait_ge(stored, 16 * GROUPS)
            sp.wait_ge(feat_zero, 1)

            def fetch(i, grp, half):
                wait(sp, tok_ps, 2 * i)
                sp.dma_start(feat[0:FR, :], feat_dram[grp, :, half * TOK:(half + 1) * TOK]).then_inc(feat_in, 16)

            def store(i):
                sp.wait_ge(y_pool, 40 * i + 40)
                for b2 in range(2):
                    dst = out[2 * i + b2, :, :].rearrange("(h d) c -> d h c", d=KD)
                    sp.dma_start(dst, o[64 * b2:64 * b2 + 64, :, :]).then_inc(stored, 16)

            fetch(0, 0, 0)
            fetch(1, 0, 1)
            with sp.Fori(1, PAIRS - 1, 2) as i:
                sp_grp = (i + 1) // 2
                fetch(i + 1, sp_grp, 0)
                store(i - 1)
                fetch(i + 2, sp_grp, 1)
                store(i)
            store(PAIRS - 2)
            store(PAIRS - 1)
            sp.wait_ge(stored, 16 * GROUPS + 32 * PAIRS)

        @block.tensor
        def _(pe):
            wsl = {"wv": wsp[:, LAYOUT["wv"][0]:LAYOUT["wv"][1]],
                   "rw1": wsp[:, LAYOUT["rw1"][0]:LAYOUT["rw1"][1]],
                   "e1": wsp[:, LAYOUT["e1"][0]:LAYOUT["e1"][1]]}

            def both(dst, weights, high, low):
                pe.matmul(dst, weights, high, start=True, stop=False)
                return pe.matmul(dst, weights, low, start=False, stop=True)

            def scores(i, par, c):
                n, mm = c // 4, c % 4
                if mm == 0:
                    pe.wait_ge(glo, HP * i + n + 1)
                wait(pe, expd, SLOTS * i + c - 3)
                both(s_bank[mm][:, :], g[:, n % 2, mm * 128:(mm + 1) * 128],
                     kh[:, par, n // HEADS, :], kl[:, par, n // HEADS, :]).then_inc(score, 1)

            def queries(i, par, n):
                wait(pe, glo, HP * i + n)
                if n == 0:
                    wait(pe, kl_sb, 4 * i + 4)
                both(g_bank[:, :], qk[:, n % HEADS, :], kh[:, par, n // HEADS, :],
                     kl[:, par, n // HEADS, :]).then_inc(gps, 1)

            def pv(i, c):
                n, mm = c // 4, c % 4
                if mm == 0:
                    pe.wait_ge(wozd, HP * i + n + 1)
                    wait(pe, mevd, HP * i + n)
                for jj in range(4):
                    last = pe.matmul(m_bank[:, jj * C:(jj + 1) * C], p[:, c % 8, jj * 128:(jj + 1) * 128],
                                     woz[:, n % 2, mm, :], start=(mm == 0 and jj == 0), stop=(mm == 3 and jj == 3),
                                     skip_group_check=True)
                last.then_inc(pvd, 1)

            def prep(kk, par, slot):
                for c in range(2):
                    if slot == P_H1[c]:
                        if c == 0:
                            pe.wait_ge(feat_in, 16 * kk + 16)
                        else:
                            pe.wait_ge(h1_sb, 2 * kk + 1)
                        pe.matmul(r_bank[:, :], k("w1"), feat[:, c * S:(c + 1) * S], start=True,
                                  stop=True).then_inc(h1_ps, 1)
                    if slot == P_TOK[c]:
                        pe.wait_ge(h1_sb, 2 * kk + 2)
                        if c:
                            pe.wait_ge(tok_sb, 2 * kk + 1)
                        for t in range(4):
                            cols = slice((4 * c + t) * 128, (4 * c + t + 1) * 128)
                            pe.matmul(r_bank[:, t * 128:(t + 1) * 128], feat[:, cols], k("wres"), start=True,
                                      stop=False, skip_group_check=True)
                            last = pe.matmul(r_bank[:, t * 128:t * 128 + C], h1t[:, cols], k("w2"), start=False,
                                             stop=True, skip_group_check=True)
                        last.then_inc(tok_ps, 1)
                    if slot == P_T[c]:
                        if c == 0:
                            pe.wait_ge(ln_pool[1], 5 * kk + 5)
                        else:
                            pe.wait_ge(kl_sb, 4 * kk + 2)
                        for t in range(4):
                            src = xn[:, 4 * c + t, :, :].rearrange("q a c -> q (a c)")
                            last = pe.transpose(r_bank[:, t * 128:(t + 1) * 128], src, k("ident"))
                        last.then_inc(t_ps, 1)
                    if slot == P_V[c]:
                        if c == 0:
                            pe.wait_ge(kl_sb, 4 * kk + 4)
                        else:
                            pe.wait_ge(v_sb, 4 * kk + 2)
                        def by_value_row(x):
                            return x[:, par, c, :].rearrange("q (a b) -> q b a", a=8)
                        both(r_bank[:, :], wsl["wv"], by_value_row(kh), by_value_row(kl)).then_inc(v_ps, 1)

            def ffn(i, par, slot):
                if slot == F_FIN:
                    pe.wait_ge(mevd, HP * i + HP)
                    for jj in range(4):
                        for b2 in range(2):
                            last = pe.matmul(f_bank[64 * b2:64 * b2 + 64, :], v[:, par, b2, jj, :],
                                             m[:, par, b2, jj, :, :], start=(jj == 0), stop=(jj == 3))
                    last.then_inc(fin_ps, 1)
                for c in range(2):
                    if slot == F_T[c]:
                        if c == 0:
                            pe.wait_ge(ln_pool[2], 5 * i + 5)
                        else:
                            pe.wait_ge(xl_sb, 2 * i + 1)
                        for t in range(4):
                            src = x2[:, 4 * c + t, :, :].rearrange("q a c -> q (a c)")
                            last = pe.transpose(f_bank[:, t * 128:(t + 1) * 128], src, k("ident"))
                        last.then_inc(x2t_ps, 1)
                    if slot == F_R[c]:
                        pe.wait_ge(xl_sb, 2 * i + 2)
                        if c:
                            pe.wait_ge(rh_sb, 2 * i + 1)
                        both(f_bank[:, :], wsl["rw1"], xh[:, c * S:(c + 1) * S],
                             xl[:, c * S:(c + 1) * S]).then_inc(rh_ps, 1)
                if slot == F_L:
                    pe.wait_ge(rh_sb, 2 * i + 2)
                    for t in range(8):
                        last = pe.matmul(f_bank[:, t * NE:(t + 1) * NE], rh[:, t * 128:(t + 1) * 128], k("rw2"),
                                         start=True, stop=True)
                    last.then_inc(l_ps, 1)
                for c in range(2):
                    for e in range(EP):
                        if slot == F_H1[c, e]:
                            if c == 0 and e == 0:
                                pe.wait_ge(gate, GATE * i + 2)
                            elif e:
                                pe.wait_ge(e1_sb, 6 * i + 3 * c + e)
                            else:
                                pe.wait_ge(e2_sb, 6 * i + 3)
                            both(f_bank[:, :], wsl["e1"][:, e * 128:(e + 1) * 128], xh[:, c * S:(c + 1) * S],
                                 xl[:, c * S:(c + 1) * S]).then_inc(e1_ps, 1)
                        if slot == F_H2[c, e]:
                            if e == 0:
                                pe.wait_ge(e1_sb, 6 * i + 3 * c + 3)
                            else:
                                pe.wait_ge(e2_sb, 6 * i + 3 * c + e)
                            pe.matmul(f_bank[:, :], k("e2")[:, e * 128:(e + 1) * 128], e1t[:, e, :], start=True,
                                      stop=True).then_inc(e2_ps, 1)

            def ffn_out(i, slot, prepped):
                for t in range(8):
                    if slot == F_Y[t]:
                        if t == 0:
                            if prepped:
                                pe.wait_ge(v_sb, 4 * (i + 2) + 4)
                            else:
                                wait(pe, y_sb, 8 * i)
                        else:
                            pe.wait_ge(y_sb, 8 * i + t)
                        if t % 4 == 0:
                            pe.wait_ge(e2_sb, 6 * i + 3 * (t // 4) + 3)
                        for e in range(EP):
                            last = pe.matmul(r_bank[:, e * 128:(e + 1) * 128], e2t[:, e, t * 128:(t + 1) * 128],
                                             k("e3")[:, e * 128:(e + 1) * 128], start=True, stop=True)
                        last.then_inc(y_ps, 1)

            def body(i, par, prev, nxt):
                for slot in range(SLOTS):
                    scores(i, par, slot)
                    if slot % 4 == 0 and (slot + 4 < SLOTS or nxt):
                        if slot + 4 < SLOTS:
                            queries(i, par, slot // 4 + 1)
                        else:
                            queries(i + 1, 1 - par, 0)
                    if slot >= LAG:
                        pv(i, slot - LAG)
                    elif prev:
                        pv(i - 1, SLOTS + slot - LAG)
                    if nxt:
                        prep(i + 1, 1 - par, slot)
                    if prev:
                        ffn(i - 1, 1 - par, slot)
                        ffn_out(i - 1, slot, nxt)

            pe.wait_ge(load_cst, 16)
            pe.wait_ge(load_cst2, 16)
            for n in range(HEADS):
                pe.matmul(s_bank[n // 4][:, (n % 4) * 128:(n % 4 + 1) * 128], k("wq")[:, n * 128:(n + 1) * 128],
                          k("wk"), start=True, stop=True).then_inc(qk_ps, 1)
            pe.wait_ge(wsplit, 2)
            for slot in range(P_V[1] + 1):
                prep(0, 0, slot)
            pe.wait_ge(qk_lo, 2)
            queries(0, 0, 0)
            body(0, 0, False, True)
            with pe.Fori(1, PAIRS - 1, 2) as i:
                body(i, 1, True, True)
                body(i + 1, 0, True, True)
            body(PAIRS - 1, 1, True, False)
            for slot in range(SLOTS):
                if slot < LAG:
                    pv(PAIRS - 1, SLOTS + slot - LAG)
                ffn(PAIRS - 1, 1, slot)
                ffn_out(PAIRS - 1, slot, False)

        @block.scalar
        def _(act):
            def exps(i, c):
                act.wait_ge(maxed, SLOTS * i + c + 1)
                wait(act, pvd, SLOTS * i + c - 7)
                nc.scalar.activation(p[:, c % 8, :], s_bank[c % 4][:, :], ACT.Exp, bias=nmax[:, c % 8:c % 8 + 1],
                                     accum_out=z[:, c % 8:c % 8 + 1]).then_inc(expd, 1)

            def queries_high(i, n):
                act.wait_ge(gps, HP * i + n + 1)
                nc.scalar.copy(g[:, n % 2, :], g_bank[:, :]).then_inc(ghi, 1)

            def prep(kk, par, slot):
                for c in range(2):
                    if slot == P_H1[c] + 1:
                        act.wait_ge(h1_ps, 2 * kk + c + 1)
                        nc.scalar.activation(h1t[:, c * S:(c + 1) * S], r_bank[:, :], ACT.Relu).then_inc(h1_sb, 1)
                    if slot == P_T[c] + 1:
                        act.wait_ge(t_ps, 2 * kk + c + 1)
                        for b2 in range(2):
                            nc.scalar.copy(keys(kh, par, b2, c), turned(b2)).then_inc(kh_sb, 1)
                    if slot == P_V[c] + 1:
                        act.wait_ge(v_ps, 2 * kk + c + 1)
                        src = r_bank[:, :].rearrange("q (a b d) -> q a b d", b=2, d=C)
                        nc.scalar.copy(v[0:64, par, c, :, :], src[0:64, :, 0, :]).then_inc(v_sb, 1)
                        nc.scalar.copy(v[64:128, par, c, :, :], src[64:128, :, 1, :]).then_inc(v_sb, 1)

            def ffn(i, slot):
                for c in range(2):
                    if slot == F_T[c] + 1:
                        act.wait_ge(x2t_ps, 2 * i + c + 1)
                        nc.scalar.copy(xh[:, c * S:(c + 1) * S], f_bank[:, :]).then_inc(xh_sb, 1)
                    if slot == F_R[c] + 1:
                        act.wait_ge(rh_ps, 2 * i + c + 1)
                        nc.scalar.activation(rh[:, c * S:(c + 1) * S], f_bank[:, :], ACT.Relu,
                                             bias=k("rb1")).then_inc(rh_sb, 1)
                    for e in range(EP):
                        if slot == F_H1[c, e] + 1:
                            act.wait_ge(e1_ps, 6 * i + 3 * c + e + 1)
                            nc.scalar.activation(e1t[:, e, :], f_bank[:, :], ACT.Relu,
                                                 bias=k("e1b")[:, e:e + 1]).then_inc(e1_sb, 1)
                if slot == F_GATE - 1:
                    act.wait_ge(gate, GATE * i + 2)
                    nc.scalar.activation(gt[:, 1, :, :], gt[:, 0, :, :], ACT.Exp).then_inc(gate_act, 1)
                if slot == F_GATE + 5:
                    act.wait_ge(gate, GATE * i + 16)
                    nc.scalar.activation(gs[:, 7, :], gs[:, 6, :], ACT.Exp).then_inc(gate_act, 1)

            def body(i, par, prev, nxt):
                for slot in range(SLOTS):
                    exps(i, slot)
                    if slot % 4 == 1:
                        if slot + 4 < SLOTS:
                            queries_high(i, slot // 4 + 1)
                        elif nxt:
                            queries_high(i + 1, 0)
                    if nxt:
                        prep(i + 1, 1 - par, slot)
                    if prev:
                        ffn(i - 1, slot)

            def keys(t, par, b2, c):
                return t[:, par, b2, :].rearrange("q (d hh) -> q d hh", d=8)[:, :, 32 * c:32 * c + 32].rearrange(
                    "q d (h e) -> q d h e", h=4)

            def turned(b2):
                return r_bank[:, :].rearrange("q (h b e d) -> q b d h e", h=4, b=2, e=8)[:, b2, :, :, :]

            act.wait_ge(angle, 9)
            nc.scalar.activation(turns[:, :], ang[:, :], ACT.Sin).then_inc(sine, 1)
            for q in range(2):
                act.wait_ge(qk_ps, 4 * q + 4)
                nc.scalar.activation(qk[:, 4 * q:4 * q + 4, :], s_bank[q][:, :].rearrange("q (n c) -> q n c", n=4),
                                     ACT.Copy, scale=SCORE_SCALE).then_inc(qk_hi, 1)
            for slot in range(P_V[1] + 2):
                prep(0, 0, slot)
            queries_high(0, 0)
            body(0, 0, False, True)
            with act.Fori(1, PAIRS - 1, 2) as i:
                body(i, 1, True, True)
                body(i + 1, 0, True, True)
            body(PAIRS - 1, 1, True, False)
            for slot in range(SLOTS):
                ffn(PAIRS - 1, slot)

        @block.vector
        def _(dve):
            def maxima(i, c):
                dve.wait_ge(score, SLOTS * i + c + 1)
                nc.vector.tensor_reduce(nmax[:, c % 8:c % 8 + 1], s_bank[c % 4][:, :], AX.X, ALU.max,
                                        negate=True).then_inc(maxed, 1)

            def queries_low(i, n):
                dve.wait_ge(ghi, HP * i + n + 1)
                nc.vector.tensor_tensor(g[64:128, n % 2, :], g_bank[64:128, :], g[64:128, n % 2, :].bitcast(F32),
                                        ALU.subtract).then_inc(glo, 1)

            def recip_sums(i, n):
                dve.wait_ge(expd, SLOTS * i + 4 * n + 4)
                q = n % 2
                nc.vector.reciprocal(rz[:, 4 * q:4 * q + 4], z[:, 4 * q:4 * q + 4]).then_inc(rzd, 1)

            def copy_m(i, par, n):
                dve.wait_ge(pvd, SLOTS * i + 4 * n + 4)
                nc.vector.tensor_copy(m[:, par, n // HEADS, :, n % HEADS, :],
                                      m_bank[:, 0:4 * C].rearrange("q (j c) -> q j c", j=4)).then_inc(mevd, 1)

            def mean(n, i, x):
                nc.vector.tensor_reduce(st[n][:, 0, :], x, AX.X, ALU.add).then_inc(ln_dve[n], 1)
                dve.wait_ge(ln_dve[n], LN_DVE * i + 1)
                nc.vector.tensor_scalar(st[n][:, 1, :], st[n][:, 0, :], -1.0 / C, None,
                                        ALU.mult).then_inc(ln_dve[n], 1)

            def rstd(n, i):
                dve.wait_ge(ln_pool[n], LN_POOL[n] * i + 2)
                nc.vector.tensor_reduce(st[n][:, 2, :], sq[n][:, :, :], AX.X, ALU.add).then_inc(ln_dve[n], 1)
                dve.wait_ge(ln_dve[n], LN_DVE * i + 3)
                nc.vector.tensor_scalar(st[n][:, 3, :], st[n][:, 2, :], 1.0 / C, LN_EPS, ALU.mult,
                                        ALU.add).then_inc(ln_dve[n], 1)

            def keys(t, par, b2, c):
                return t[:, par, b2, :].rearrange("q (d hh) -> q d hh", d=8)[:, :, 32 * c:32 * c + 32].rearrange(
                    "q d (h e) -> q d h e", h=4)

            def turned(b2):
                return r_bank[:, :].rearrange("q (h b e d) -> q b d h e", h=4, b=2, e=8)[:, b2, :, :, :]

            def prep(kk, par, slot):
                for c in range(2):
                    if slot == P_TOK[c] + 1:
                        dve.wait_ge(tok_ps, 2 * kk + c + 1)
                        nc.vector.tensor_copy(tok[:, 4 * c:4 * c + 4, :],
                                              r_bank[:, :].rearrange("q (t c) -> q t c", t=4)).then_inc(tok_sb, 1)
                    if slot == P_T[c] + 1:
                        for b2 in range(2):
                            dve.wait_ge(kh_sb, 4 * kk + 2 * c + 2)
                            nc.vector.tensor_tensor(keys(kl, par, b2, c), turned(b2),
                                                    keys(kh, par, b2, c).bitcast(F32),
                                                    ALU.subtract).then_inc(kl_sb, 1)
                if slot == P_LNA:
                    dve.wait_ge(tok_sb, 2 * kk + 2)
                    mean(0, kk, tok[:, :, 0:C])
                if slot == P_LNA2:
                    rstd(0, kk)
                if slot == P_LNB:
                    dve.wait_ge(ln_pool[0], 6 * kk + 6)
                    nc.vector.scalar_tensor_tensor(out=h[:, par, :, :], in0=tok[:, :, C:], scalar=0.1,
                                                   in1=xc[0][:, :, :], op0=ALU.mult, op1=ALU.add).then_inc(h_sb, 1)
                    dve.wait_ge(h_sb, kk + 1)
                    mean(1, kk, h[:, par, :, :])
                if slot == P_LNB2:
                    rstd(1, kk)

            def bcast(x):
                return x.unsqueeze(2).to_broadcast([128, 8, NE])

            def gating(i, part):
                base = GATE * i

                def done(n, ins):
                    ins.then_inc(gate, 1)

                def after(n):
                    dve.wait_ge(gate, base + n)

                rank = k("rank").unsqueeze(1).to_broadcast([128, 8, NE])
                logits = f_bank[:, 0:8 * NE].rearrange("q (t e) -> q t e", t=8)
                G, V = (lambda n: gt[:, n, :, :]), (lambda n: gs[:, n, :])
                tt, red = nc.vector.tensor_tensor, nc.vector.tensor_reduce
                if part == 0:
                    dve.wait_ge(l_ps, i + 1)
                    done(1, red(V(0), logits, AX.X, ALU.max))
                    after(1)
                    done(2, tt(G(0), logits, bcast(V(0)), ALU.subtract))
                if part == 1:
                    dve.wait_ge(gate_act, 2 * i + 1)
                    done(3, red(V(1), G(1), AX.X, ALU.add))
                    after(3)
                    done(4, nc.vector.reciprocal(V(2), V(1)))
                    after(4)
                    done(5, tt(G(2), G(1), bcast(V(2)), ALU.mult))
                if part == 2:
                    after(5)
                    done(6, red(V(3), G(2), AX.X, ALU.max))
                    after(6)
                    done(7, tt(G(3), G(2), bcast(V(3)), ALU.is_equal))
                    after(7)
                    done(8, tt(G(3), G(3), rank, ALU.mult))
                if part == 3:
                    after(8)
                    done(9, red(V(4), G(3), AX.X, ALU.max))
                    after(9)
                    done(10, tt(G(4), G(3), bcast(V(4)), ALU.is_equal))
                    after(10)
                    done(11, nc.vector.scalar_tensor_tensor(out=G(5), in0=G(4), scalar=-2.0, in1=G(2), op0=ALU.mult,
                                                            op1=ALU.add))
                if part == 4:
                    after(11)
                    done(12, red(V(5), G(5), AX.X, ALU.max))
                    after(12)
                    done(13, tt(G(6), G(5), bcast(V(5)), ALU.is_equal))
                    after(13)
                    done(14, tt(G(6), G(6), rank, ALU.mult))
                    after(14)
                    done(15, red(V(8), G(6), AX.X, ALU.max))
                    done(16, tt(V(6), V(5), V(3), ALU.subtract))
                if part == 5:
                    after(15)
                    done(17, tt(G(7), G(6), bcast(V(8)), ALU.is_equal))
                    dve.wait_ge(gate_act, 2 * i + 2)
                    done(18, nc.vector.tensor_scalar(V(9), V(7), 1.0, None, ALU.add))
                    after(18)
                    done(19, nc.vector.reciprocal(V(0), V(9)))
                    after(19)
                    done(20, tt(V(1), V(7), V(0), ALU.mult))
                if part == 6:
                    after(20)
                    tt(G(0), G(4), bcast(V(0)), ALU.mult).then_inc(gate, 1)
                    tt(G(1), G(7), bcast(V(1)), ALU.mult).then_inc(gate, 1)
                    after(22)
                    tt(G(8), G(0), G(1), ALU.add).then_inc(gated, 1)

            def ffn(i, par, slot):
                if slot == F_LN:
                    dve.wait_ge(fin_ps, i + 1)
                    nc.vector.tensor_tensor(hatt[:, :, :], h[:, par, :, :],
                                            f_bank[:, :].rearrange("q (t c) -> q t c", t=8),
                                            ALU.add).then_inc(hatt_sb, 1)
                    dve.wait_ge(hatt_sb, i + 1)
                    mean(2, i, hatt[:, :, :])
                if slot == F_LN2:
                    rstd(2, i)
                for c in range(2):
                    if slot == F_T[c] + 1:
                        dve.wait_ge(xh_sb, 2 * i + c + 1)
                        nc.vector.tensor_tensor(xl[:, c * S:(c + 1) * S], f_bank[:, :],
                                                xh[:, c * S:(c + 1) * S].bitcast(F32),
                                                ALU.subtract).then_inc(xl_sb, 1)
                    for e in range(EP):
                        if slot == F_H2[c, e] + 1:
                            dve.wait_ge(e2_ps, 6 * i + 3 * c + e + 1)
                            nc.vector.tensor_scalar(e2t[:, e, c * S:(c + 1) * S], f_bank[:, :],
                                                    k("e2b")[:, e:e + 1], 0.0, ALU.add, ALU.max).then_inc(e2_sb, 1)
                if slot == F_L + 1:
                    gating(i, 0)
                for part in range(1, 7):
                    if slot == F_GATE + part - 1 + (part > 4):
                        gating(i, part)
                for t in range(8):
                    if slot == F_Y[t] + 1:
                        dve.wait_ge(y_ps, 8 * i + t + 1)
                        if t >= 2:
                            dve.wait_ge(y_pool, 40 * i + 5 * t - 5)
                        nc.vector.tensor_tensor(y[:, t % 2, :, :].rearrange("q e c -> q (e c)"), r_bank[:, 0:NE * C],
                                                k("e3b"), ALU.add).then_inc(y_sb, 1)

            def body(i, par, prev, nxt):
                for slot in range(SLOTS):
                    maxima(i, slot)
                    if slot % 4 == 2:
                        if slot + 4 < SLOTS:
                            queries_low(i, slot // 4 + 1)
                        elif nxt:
                            queries_low(i + 1, 0)
                    if slot % 4 == 1:
                        if slot >= 4:
                            recip_sums(i, slot // 4 - 1)
                        elif prev:
                            recip_sums(i - 1, HP - 1)
                    if slot % 4 == 3:
                        if slot >= LAG + 4:
                            copy_m(i, par, (slot - LAG) // 4 - 1)
                        elif prev:
                            copy_m(i - 1, 1 - par, HP + (slot - LAG) // 4 - 1)
                    if nxt:
                        prep(i + 1, 1 - par, slot)
                    if prev:
                        ffn(i - 1, 1 - par, slot)

            def four(n):
                return cst[:, LAYOUT["fourier"][0] + n:LAYOUT["fourier"][0] + n + 1]
            period, harm, phase, quarter, shift, amp, one = (four(n) for n in range(7))
            two_pi = float(np.float32(2.0 * math.pi))
            c1 = 6.28125
            c2 = float(np.float32(int((2 * math.pi - c1) * 2 ** 21)) / 2 ** 21)
            c3 = float(np.float32(2 * math.pi - c1 - c2))
            magic = 1.5 * 2 ** 23
            pi = 3.1415925
            dve.wait_ge(load_ids, 16)
            dve.wait_ge(load_cst, 16)
            A, T = ang[:, :], turns[:, :]
            ts, stt = nc.vector.tensor_scalar, nc.vector.scalar_tensor_tensor
            nc.vector.memset(feat[:, :], 0.0).then_inc(feat_zero, 1)
            nc.vector.reciprocal(per_turn[:, :], period).then_inc(inverse, 1)
            dve.wait_ge(inverse, 1)
            ts(A, ids_sb[:, :], two_pi, per_turn[:, 0:1], ALU.mult, ALU.mult).then_inc(angle, 1)
            dve.wait_ge(angle, 1)
            ts(A, A, harm, phase, ALU.mult, ALU.add).then_inc(angle, 1)
            dve.wait_ge(angle, 2)
            ts(T, A, 1.0 / (2.0 * math.pi), quarter, ALU.mult, ALU.add).then_inc(angle, 1)
            dve.wait_ge(angle, 3)
            ts(T, T, magic, magic, ALU.add, ALU.subtract).then_inc(angle, 1)
            for n, cn in enumerate((c1, c2, c3)):
                dve.wait_ge(angle, 4 + n)
                stt(out=A, in0=T, scalar=-cn, in1=A, op0=ALU.mult, op1=ALU.add).then_inc(angle, 1)
            dve.wait_ge(angle, 7)
            ts(A, A, shift, pi, ALU.add, ALU.min).then_inc(angle, 1)
            dve.wait_ge(angle, 8)
            ts(A, A, -pi, None, ALU.max).then_inc(angle, 1)
            nc.vector.tensor_copy(wsp[:, :], cst[:, 0:SPLIT]).then_inc(wsplit, 1)
            dve.wait_ge(wsplit, 1)
            nc.vector.tensor_tensor(wsp[64:128, :], cst[64:128, 0:SPLIT], wsp[64:128, :].bitcast(F32),
                                    ALU.subtract).then_inc(wsplit, 1)
            dve.wait_ge(sine, 1)
            ts(A, T, amp, one, ALU.mult, ALU.add).then_inc(feats, 1)
            for q in range(2):
                dve.wait_ge(qk_hi, q + 1)
                stt(out=qk[64:128, 4 * q:4 * q + 4, :].rearrange("q n c -> q (n c)"), in0=s_bank[q][64:128, :],
                    scalar=SCORE_SCALE, in1=qk[64:128, 4 * q:4 * q + 4, :].rearrange("q n c -> q (n c)").bitcast(F32),
                    op0=ALU.mult, op1=ALU.subtract).then_inc(qk_lo, 1)
            for slot in range(P_V[1] + 2):
                prep(0, 0, slot)
            queries_low(0, 0)
            body(0, 0, False, True)
            with dve.Fori(1, PAIRS - 1, 2) as i:
                body(i, 1, True, True)
                body(i + 1, 0, True, True)
            body(PAIRS - 1, 1, True, False)
            for slot in range(SLOTS):
                if slot == 1:
                    recip_sums(PAIRS - 1, HP - 1)
                if slot in (3, 7):
                    copy_m(PAIRS - 1, 1, HP + (slot - LAG) // 4 - 1)
                ffn(PAIRS - 1, 1, slot)

        @block.gpsimd
        def _(pool):
            def over_sums(i, n):
                pool.wait_ge(rzd, HP * i + n + 1)
                q = n % 2
                nc.gpsimd.tensor_tensor(woz[:, q, :, :], k("wo").rearrange("q (m c) -> q m c", m=4),
                                        rz[:, 4 * q:4 * q + 4].unsqueeze(2).to_broadcast([128, 4, C]),
                                        ALU.mult).then_inc(wozd, 1)

            def wide(x):
                return x.unsqueeze(2).to_broadcast([128, 8, C])

            def centre(n, i, x):
                pool.wait_ge(ln_dve[n], LN_DVE * i + 2)
                nc.gpsimd.tensor_tensor(xc[n][:, :, :], x, wide(st[n][:, 1, :]), ALU.add).then_inc(ln_pool[n], 1)
                pool.wait_ge(ln_pool[n], LN_POOL[n] * i + 1)
                nc.gpsimd.tensor_tensor(sq[n][:, :, :], xc[n][:, :, :], xc[n][:, :, :],
                                        ALU.mult).then_inc(ln_pool[n], 1)

            def normalise(n, i, *dsts):
                pool.wait_ge(ln_dve[n], LN_DVE * i + 4)
                nc.gpsimd.tensor_tensor(st[n][:, 4, :], st[n][:, 3, :], power[:, :], ALU.pow).then_inc(ln_pool[n], 1)
                pool.wait_ge(ln_pool[n], LN_POOL[n] * i + 3)
                for dst in dsts:
                    nc.gpsimd.tensor_tensor(dst, xc[n][:, :, :], wide(st[n][:, 4, :]),
                                            ALU.mult).then_inc(ln_pool[n], 1)

            def prep(kk, par, slot):
                if slot == P_LNA:
                    centre(0, kk, tok[:, :, 0:C])
                if slot == P_LNA2:
                    normalise(0, kk, xc[0][:, :, :])
                    pool.wait_ge(ln_pool[0], 6 * kk + 4)
                    for n, (w, op) in enumerate((("gamma", ALU.mult), ("beta", ALU.add))):
                        nc.gpsimd.tensor_tensor(xc[0][:, :, :], xc[0][:, :, :],
                                                k(w).unsqueeze(1).to_broadcast([128, 8, C]), op).then_inc(ln_pool[0], 1)
                        if n == 0:
                            pool.wait_ge(ln_pool[0], 6 * kk + 5)
                if slot == P_LNB:
                    centre(1, kk, h[:, par, :, :])
                if slot == P_LNB2:
                    normalise(1, kk, xn[:, :, 0, :], xn[:, :, 1, :])

            def ffn(i, slot):
                if slot == F_LN:
                    centre(2, i, hatt[:, :, :])
                if slot == F_LN2:
                    normalise(2, i, x2[:, :, 0, :], x2[:, :, 1, :])
                for t in range(8):
                    if slot == F_Y[t] + 1:
                        base = 40 * i + 5 * t
                        if t == 0:
                            pool.wait_ge(gated, i + 1)
                            pool.wait_ge(stored, 16 * GROUPS + 32 * i)
                        pool.wait_ge(y_sb, 8 * i + t + 1)
                        yt, s2 = y[:, t % 2, :, :], ys[:, t % 2, :, :]
                        tt = nc.gpsimd.tensor_tensor
                        tt(yt, yt, gt[:, 8, t, :].unsqueeze(2).to_broadcast([128, NE, C]),
                           ALU.mult).then_inc(y_pool, 1)
                        pool.wait_ge(y_pool, base + 1)
                        tt(s2[:, 0:3, :], yt[:, 0:3, :], yt[:, 3:6, :], ALU.add).then_inc(y_pool, 1)
                        pool.wait_ge(y_pool, base + 2)
                        tt(s2[:, 3, :], s2[:, 0, :], s2[:, 1, :], ALU.add).then_inc(y_pool, 1)
                        tt(s2[:, 2, :], s2[:, 2, :], hatt[:, t, :], ALU.add).then_inc(y_pool, 1)
                        pool.wait_ge(y_pool, base + 4)
                        tt(o[:, t, :], s2[:, 2, :], s2[:, 3, :], ALU.add).then_inc(y_pool, 1)

            def body(i, par, prev, nxt):
                for slot in range(SLOTS):
                    if slot % 4 == 1:
                        if slot >= 4:
                            over_sums(i, slot // 4 - 1)
                        elif prev:
                            over_sums(i - 1, HP - 1)
                    if nxt:
                        prep(i + 1, 1 - par, slot)
                    if prev:
                        ffn(i - 1, slot)

            nc.gpsimd.memset(power[:, :], -0.5).then_inc(power_set, 1)
            pool.wait_ge(power_set, 1)
            pool.wait_ge(load_cst2, 16)
            for slot in range(P_V[1] + 2):
                prep(0, 0, slot)
            body(0, 0, False, True)
            with pool.Fori(1, PAIRS - 1, 2) as i:
                body(i, 1, True, True)
                body(i + 1, 0, True, True)
            body(PAIRS - 1, 1, True, False)
            for slot in range(SLOTS):
                if slot == 1:
                    over_sums(PAIRS - 1, HP - 1)
                ffn(PAIRS - 1, slot)


def laid_out(x):
    w = {n[3:]: np.asarray(a) for n, a in x.items() if n.startswith("L0_")}

    def rows(a):
        a = np.asarray(a, np.float32)
        a = a.reshape(a.shape[0], -1)
        return np.concatenate([a, np.zeros((128 - a.shape[0], a.shape[1]), np.float32)], 0)

    def every_row(a):
        return np.repeat(a.reshape(1, -1), 128, 0)

    def diagonal(a):
        d = np.zeros((EP, 2, a.shape[1], 2, a.shape[2]), np.float32)
        for e in range(2):
            d[:, e, :, e, :] = a[e::2]
        return d.transpose(1, 2, 0, 3, 4).reshape(2 * a.shape[1], -1)

    def cols(a):
        return a.reshape(EP, 2 * C).T

    parts = {}
    parts["wv"] = np.tile(w["attn_Wv"].T, (2, 2))
    r1 = np.tile(w["ffn_router_w1"], (2, 1))
    parts["rw1"] = np.concatenate([r1, np.zeros((128, 128 - r1.shape[1]), np.float32)], 1)
    parts["e1"] = np.tile(w["ffn_expert_w1"].transpose(1, 0, 2).reshape(C, -1), (2, 1))
    wq = w["attn_Wq"].reshape(HEADS, KD, C).transpose(1, 0, 2)
    parts["wq"] = rows(np.concatenate([wq, wq], 2))
    parts["wk"] = rows(np.tile(w["attn_Wk"], (1, 2)))
    wo = w["attn_Wo"].T.reshape(C, 8, C).transpose(1, 0, 2).reshape(4, 128, C)
    parts["wo"] = wo.transpose(1, 0, 2).reshape(128, -1)
    parts["w1"] = rows(np.concatenate([w["tok_W1"], w["tok_b1"].reshape(1, -1)], 0))
    zero = np.zeros((FD, C), np.float32)
    parts["wres"] = rows(np.concatenate([
        np.concatenate([zero, w["tok_b2"].reshape(1, -1)], 0),
        np.concatenate([w["tok_Wres"], w["tok_bres"].reshape(1, -1)], 0)], 1))
    parts["w2"] = w["tok_W2"]
    parts["gamma"], parts["beta"] = every_row(w["tok_gamma"]), every_row(w["tok_beta"])
    one = np.ones(1, np.float32)
    parts["rw2"] = rows(np.concatenate([w["ffn_router_w2"], w["ffn_router_b2"].reshape(1, -1)], 0))
    parts["rb1"] = rows(np.concatenate([w["ffn_router_b1"], one]).reshape(-1, 1))
    parts["e1b"], parts["e2b"] = cols(w["ffn_expert_b1"]), cols(w["ffn_expert_b2"])
    parts["e2"], parts["e3"] = diagonal(w["ffn_expert_w2"]), diagonal(w["ffn_expert_w3"])
    parts["e3b"] = every_row(w["ffn_expert_b3"])
    parts["ident"] = np.eye(128, dtype=np.float32)
    parts["rank"] = every_row(np.arange(NE, 0, -1, dtype=np.float32))

    n = len(PERIODS)
    f = np.zeros((32, 7), np.float32)
    f[:, 0] = 1.0
    f[:FD, 0] = np.repeat(np.array(PERIODS, np.float32), 2 * HARM)
    f[:FD, 1] = np.tile(np.repeat(np.arange(1, HARM + 1, dtype=np.float32), 2), n)
    f[:FD, 2] = np.repeat(w["tok_ph"].reshape(-1), 2)
    f[:FD, 3] = np.tile(np.array([0.0, 0.25], np.float32), n * HARM)
    f[:FD, 4] = np.tile(np.array([0.0, math.pi / 2], np.float32), n * HARM)
    f[:FD, 5] = np.repeat(w["tok_hw"].reshape(-1), 2)
    f[FD, 6] = 1.0
    parts["fourier"] = np.tile(f, (GROUPS, 1))

    consts = np.zeros((128, WIDTH), np.float32)
    for name, (a, b) in LAYOUT.items():
        consts[:, a:b] = parts[name]

    t = np.stack([np.asarray(x[name]) for name in ("x", "itok_BS_0_23", "itok_BS_0_11", "itok_BS_0_30")])
    t = t.reshape(n, GROUPS, 2, 2, HEADS, KD).transpose(1, 0, 2, 4, 3, 5).reshape(GROUPS, n, GCOL)
    ids = np.zeros((GROUPS, 32, GCOL), t.dtype)
    ids[:, :FD] = np.repeat(t, 2 * HARM, 1)
    return ids.reshape(128, GCOL), consts


def kernel(**inputs):
    import concourse.bacc as bacc
    from concourse.bass_utils import run_bass_kernel_spmd

    ids, consts = laid_out(inputs)
    nc = bacc.Bacc("TRN2", target_bir_lowering=False, num_devices=1)
    ids_d = nc.dram_tensor("ids", ids.shape, mybir.dt.from_np(ids.dtype), kind="ExternalInput").ap()
    cst_d = nc.dram_tensor("consts", consts.shape, mybir.dt.float32, kind="ExternalInput").ap()
    out_d = nc.dram_tensor("tower_out", (B, S, C), mybir.dt.float32, kind="ExternalOutput").ap()
    tower(nc, ids_d, cst_d, out_d)
    r = run_bass_kernel_spmd(nc, [{"ids": ids, "consts": consts}], core_ids=[0])
    return r.results[0]["tower_out"]
```

```python
import math
from contextlib import ExitStack

import numpy as np
import concourse.bass as bass
from concourse import mybir

B, S, C = 16, 512, 64
HEADS, KD = 8, 64
NE = 6
EP = NE // 2
HARM, PERIODS = 3, (7.0, 24.0, 12.0, 1.0)
FD = 2 * HARM * len(PERIODS)
FR = FD + 1
PAIRS = B // 2
TOK = 2 * S
HP = 2 * HEADS
HH = HP // 2
SLOTS = 4 * HP
PV_AT, MT_AT, TURN_AT = 13, 19, 22
GROUPS = 4
GCOL = B * S // GROUPS
LN_EPS = 1e-5
SCORE_SCALE = float(np.float32(1.0) / np.sqrt(KD // HEADS).astype(np.float32))

LAYOUT, WIDTH = {}, 0
for _name, _w in (("wv", 128), ("rw1", 128), ("e1", EP * 128), ("fourier", 7), ("wq", HEADS * 128),
                  ("wk", 128), ("wo", 4 * C), ("w1", 128), ("wres", 128), ("w2", C), ("gamma", C),
                  ("beta", C), ("rw2", NE), ("rb1", 1), ("e1b", EP), ("e2", EP * 128), ("e2b", EP),
                  ("e3", EP * 128), ("e3b", NE * C), ("ident", 128), ("rank", NE)):
    LAYOUT[_name] = (WIDTH, WIDTH + _w)
    WIDTH += _w
SPLIT = LAYOUT["e1"][1]
EARLY = LAYOUT["wq"][0]

P_H1, P_TOK, P_LNA, P_LNA2, P_LNB, P_LNB2 = (0, 2), (4, 6), 7, 10, 18, 21
P_T, P_V = (25, 27), (29, 31)
F_FIN, F_LN, F_LN2, F_T, F_R, F_L = 16, 17, 21, (25, 27), (29, 31), 33
F_GATE = 35
F_H1 = {(0, 0): 35, (0, 1): 36, (0, 2): 38, (1, 0): 43, (1, 1): 45, (1, 2): 46}
F_H2 = {(0, 0): 39, (0, 1): 41, (0, 2): 42, (1, 0): 48, (1, 1): 49, (1, 2): 51}
F_Y = (44, 46, 48, 50, 53, 55, 57, 59)


def tower(nc, ids, consts, out):
    F32, F32R, I32 = mybir.dt.float32, mybir.dt.float32r, mybir.dt.int32
    ALU, ACT, AX = mybir.AluOpType, mybir.ActivationFunctionType, mybir.AxisListType

    feat_dram = nc.dram_tensor("feat_scratch", (GROUPS, FR, GCOL), F32, kind="Internal").ap()

    ctx = ExitStack()
    with ctx:
        def sb(name, shape, dt=F32):
            return ctx.enter_context(nc.sbuf_tensor(name, shape, dt))

        def pb(name):
            return ctx.enter_context(nc.psum_tensor(name, [128, 512], F32))

        def sem(name):
            return ctx.enter_context(nc.semaphore(name))

        cst = sb("cst", [128, WIDTH])

        def k(name):
            return cst[:, LAYOUT[name][0]:LAYOUT[name][1]]

        wsp = sb("wsp", [128, SPLIT], F32R)
        qk = sb("qk", [128, HEADS, 128], F32R)
        per_turn = sb("per_turn", [128, 1])
        power = sb("power", [128, 8])
        feat = sb("feat", [128, TOK])
        h1t = sb("h1t", [128, TOK])
        tok = sb("tok", [128, 8, 128])
        xc = [sb(f"xc{n}", [128, 8, C]) for n in range(3)]
        sq = [sb(f"sq{n}", [128, 8, C]) for n in range(3)]
        st = [sb(f"st{n}", [128, 5, 8]) for n in range(3)]
        h = sb("h", [128, 2, 8, C])
        xn = sb("xn", [128, 8, 2, C])
        kh = sb("kh", [128, 2, 2, S], F32R)
        kl = sb("kl", [128, 2, 2, S], F32R)
        v = sb("v", [128, 2, 2, 4, C])
        g = sb("g", [128, 2, S], F32R)
        p = sb("p", [128, 16, S])
        nmax = sb("nmax", [128, 16])
        z = sb("z", [128, 2, 8])
        rz = sb("rz", [128, 2, 8])
        woz = sb("woz", [128, 2, 8, C])
        mt = sb("mt", [128, S])
        m = sb("m", [128, 2, 2, 4, HEADS, C])
        flat = m[:, :, :, :, :, :].rearrange("q a b j n c -> q (a b j n c)")
        ang, turns, ids_sb = (flat[:, n * GCOL:(n + 1) * GCOL] for n in range(3))
        ids_sb = ids_sb.bitcast(I32)
        hatt = sb("hatt", [128, 8, C])
        x2 = sb("x2", [128, 8, 2, C])
        xh = sb("xh", [128, TOK], F32R)
        xl = sb("xl", [128, TOK], F32R)
        rh = sb("rh", [128, TOK])
        gt = sb("gt", [128, 9, 8, NE])
        gs = sb("gs", [128, 10, 8])
        e1t = sb("e1t", [128, EP, S])
        e2t = sb("e2t", [128, EP, TOK])
        y = sb("y", [128, 2, NE, C])
        ys = sb("ys", [128, 2, 4, C])
        o = sb("o", [128, 8, C])

        s_bank = [pb(f"s_bank{n}") for n in range(4)]
        m_bank, g_bank, r_bank, f_bank = pb("m_bank"), pb("g_bank"), pb("r_bank"), pb("f_bank")

        (load_ids, load_cst, load_cst2, stored, feat_in, feat_zero) = [
            sem(x) for x in ("load_ids", "load_cst", "load_cst2", "stored", "feat_in", "feat_zero")]
        (inverse, power_set, angle, sine, feats, wsplit, qk_ps, qk_hi, qk_lo) = [
            sem(x) for x in ("inverse", "power_set", "angle", "sine", "feats", "wsplit", "qk_ps", "qk_hi", "qk_lo")]
        (score, maxed, expd, rzd, wozd, pvd, mtd, turned_ps, mevd, gps, ghi, glo) = [
            sem(x) for x in ("score", "maxed", "expd", "rzd", "wozd", "pvd", "mtd", "turned_ps", "mevd", "gps", "ghi", "glo")]
        (h1_ps, h1_sb, tok_ps, tok_sb, h_sb, t_ps, kh_sb, kl_sb, v_ps, v_sb) = [
            sem(x) for x in ("h1_ps", "h1_sb", "tok_ps", "tok_sb", "h_sb", "t_ps", "kh_sb", "kl_sb", "v_ps", "v_sb")]
        ln_dve = [sem(f"ln_dve{n}") for n in range(3)]
        ln_pool = [sem(f"ln_pool{n}") for n in range(3)]
        (fin_ps, hatt_sb, x2t_ps, xh_sb, xl_sb, rh_ps, rh_sb, l_ps, gate, gate_act) = [
            sem(x) for x in ("fin_ps", "hatt_sb", "x2t_ps", "xh_sb", "xl_sb", "rh_ps", "rh_sb", "l_ps", "gate", "gate_act")]
        (e1_ps, e1_sb, e2_ps, e2_sb, y_ps, y_sb, y_pool, gated) = [
            sem(x) for x in ("e1_ps", "e1_sb", "e2_ps", "e2_sb", "y_ps", "y_sb", "y_pool", "gated")]

        LN_DVE, LN_POOL = 4, (6, 5, 5)
        GATE = 22

        def wait(eng, s, value):
            if isinstance(value, int) and value <= 0:
                return
            eng.wait_ge(s, value)

        block = ctx.enter_context(nc.Block())

        @block.sync
        def _(sp):
            sp.dma_start(ids_sb[:, :], ids).then_inc(load_ids, 16)
            sp.dma_start(cst[:, 0:EARLY], consts[:, 0:EARLY]).then_inc(load_cst, 16)
            sp.dma_start(cst[:, EARLY:], consts[:, EARLY:]).then_inc(load_cst2, 16)
            sp.wait_ge(feats, 1)
            for q in range(GROUPS):
                sp.dma_start(feat_dram[q, :, :], ang[32 * q:32 * q + FR, :]).then_inc(stored, 16)
            sp.wait_ge(stored, 16 * GROUPS)
            sp.wait_ge(feat_zero, 1)

            def fetch(i, grp, half):
                wait(sp, tok_ps, 2 * i)
                sp.dma_start(feat[0:FR, :], feat_dram[grp, :, half * TOK:(half + 1) * TOK]).then_inc(feat_in, 16)

            def store(i):
                sp.wait_ge(y_pool, 40 * i + 40)
                for b2 in range(2):
                    dst = out[2 * i + b2, :, :].rearrange("(h d) c -> d h c", d=KD)
                    sp.dma_start(dst, o[64 * b2:64 * b2 + 64, :, :]).then_inc(stored, 16)

            fetch(0, 0, 0)
            fetch(1, 0, 1)
            fetch(2, 1, 0)
            with sp.Fori(1, PAIRS - 3, 2) as i:
                fetch(i + 2, (i + 1) // 2, 1)
                store(i - 1)
                fetch(i + 3, (i + 3) // 2, 0)
                store(i)
            fetch(PAIRS - 1, GROUPS - 1, 1)
            for n in range(PAIRS - 4, PAIRS):
                store(n)
            sp.wait_ge(stored, 16 * GROUPS + 32 * PAIRS)

        @block.tensor
        def _(pe):
            wsl = {"wv": wsp[:, LAYOUT["wv"][0]:LAYOUT["wv"][1]],
                   "rw1": wsp[:, LAYOUT["rw1"][0]:LAYOUT["rw1"][1]],
                   "e1": wsp[:, LAYOUT["e1"][0]:LAYOUT["e1"][1]]}

            def both(dst, weights, high, low):
                pe.matmul(dst, weights, high, start=True, stop=False)
                return pe.matmul(dst, weights, low, start=False, stop=True)

            def scores(i, par, c):
                n, mm = c // 4, c % 4
                if mm == 0:
                    pe.wait_ge(glo, HP * i + n + 1)
                wait(pe, expd, SLOTS * i + c - 3)
                both(s_bank[mm][:, :], g[:, n % 2, mm * 128:(mm + 1) * 128],
                     kh[:, par, n // HEADS, :], kl[:, par, n // HEADS, :]).then_inc(score, 1)

            def queries(i, par, n):
                wait(pe, glo, HP * i + n)
                if n % 2 == 1:
                    wait(pe, mevd, HH * i + (n - 5) // 2)
                if n == 0:
                    wait(pe, kl_sb, 4 * i + 4)
                both(g_bank[:, :], qk[:, n % HEADS, :], kh[:, par, n // HEADS, :],
                     kl[:, par, n // HEADS, :]).then_inc(gps, 1)

            def pv(i, a, mm):
                if mm == 0:
                    pe.wait_ge(wozd, 2 * (HH * i + a) + 2)
                    wait(pe, mtd, HH * i + a)
                for hh in range(2):
                    last = pe.matmul(m_bank[64 * hh:64 * hh + 64, :], woz[:, a % 2, 4 * hh + mm, :],
                                     p[:, 8 * (a % 2) + 4 * hh + mm, :], start=(mm == 0), stop=(mm == 3))
                last.then_inc(pvd, 1)

            def turn(i, a, latest):
                pe.wait_ge(mtd, HH * i + a + 1)
                pe.wait_ge(glo, latest)
                for jj in range(4):
                    last = pe.transpose(g_bank[:, jj * 128:(jj + 1) * 128], mt[:, jj * 128:(jj + 1) * 128], k("ident"))
                last.then_inc(turned_ps, 1)

            def prep(kk, par, slot):
                for c in range(2):
                    if slot == P_H1[c]:
                        if c == 0:
                            pe.wait_ge(feat_in, 16 * kk + 16)
                        else:
                            pe.wait_ge(h1_sb, 2 * kk + 1)
                        pe.matmul(r_bank[:, :], k("w1"), feat[:, c * S:(c + 1) * S], start=True,
                                  stop=True).then_inc(h1_ps, 1)
                    if slot == P_TOK[c]:
                        pe.wait_ge(h1_sb, 2 * kk + 2)
                        if c:
                            pe.wait_ge(tok_sb, 2 * kk + 1)
                        for t in range(4):
                            cols = slice((4 * c + t) * 128, (4 * c + t + 1) * 128)
                            pe.matmul(r_bank[:, t * 128:(t + 1) * 128], feat[:, cols], k("wres"), start=True,
                                      stop=False, skip_group_check=True)
                            last = pe.matmul(r_bank[:, t * 128:t * 128 + C], h1t[:, cols], k("w2"), start=False,
                                             stop=True, skip_group_check=True)
                        last.then_inc(tok_ps, 1)
                    if slot == P_T[c]:
                        if c == 0:
                            pe.wait_ge(ln_pool[1], 5 * kk + 5)
                        else:
                            pe.wait_ge(kl_sb, 4 * kk + 2)
                        for t in range(4):
                            src = xn[:, 4 * c + t, :, :].rearrange("q a c -> q (a c)")
                            last = pe.transpose(r_bank[:, t * 128:(t + 1) * 128], src, k("ident"))
                        last.then_inc(t_ps, 1)
                    if slot == P_V[c]:
                        if c == 0:
                            pe.wait_ge(kl_sb, 4 * kk + 4)
                        else:
                            pe.wait_ge(v_sb, 4 * kk + 2)
                        def by_value_row(x):
                            return x[:, par, c, :].rearrange("q (a b) -> q b a", a=8)
                        both(r_bank[:, :], wsl["wv"], by_value_row(kh), by_value_row(kl)).then_inc(v_ps, 1)

            def ffn(i, par, slot):
                if slot == F_FIN:
                    pe.wait_ge(mevd, HH * i + HH)
                    for jj in range(4):
                        for b2 in range(2):
                            last = pe.matmul(f_bank[64 * b2:64 * b2 + 64, :], v[:, par, b2, jj, :],
                                             m[:, par, b2, jj, :, :], start=(jj == 0), stop=(jj == 3))
                    last.then_inc(fin_ps, 1)
                for c in range(2):
                    if slot == F_T[c]:
                        if c == 0:
                            pe.wait_ge(ln_pool[2], 5 * i + 5)
                        else:
                            pe.wait_ge(xl_sb, 2 * i + 1)
                        for t in range(4):
                            src = x2[:, 4 * c + t, :, :].rearrange("q a c -> q (a c)")
                            last = pe.transpose(f_bank[:, t * 128:(t + 1) * 128], src, k("ident"))
                        last.then_inc(x2t_ps, 1)
                    if slot == F_R[c]:
                        pe.wait_ge(xl_sb, 2 * i + 2)
                        if c:
                            pe.wait_ge(rh_sb, 2 * i + 1)
                        both(f_bank[:, :], wsl["rw1"], xh[:, c * S:(c + 1) * S],
                             xl[:, c * S:(c + 1) * S]).then_inc(rh_ps, 1)
                if slot == F_L:
                    pe.wait_ge(rh_sb, 2 * i + 2)
                    for t in range(8):
                        last = pe.matmul(f_bank[:, t * NE:(t + 1) * NE], rh[:, t * 128:(t + 1) * 128], k("rw2"),
                                         start=True, stop=True)
                    last.then_inc(l_ps, 1)
                for c in range(2):
                    for e in range(EP):
                        if slot == F_H1[c, e]:
                            if c == 0 and e == 0:
                                pe.wait_ge(gate, GATE * i + 2)
                            elif e:
                                pe.wait_ge(e1_sb, 6 * i + 3 * c + e)
                            else:
                                pe.wait_ge(e2_sb, 6 * i + 3)
                            both(f_bank[:, :], wsl["e1"][:, e * 128:(e + 1) * 128], xh[:, c * S:(c + 1) * S],
                                 xl[:, c * S:(c + 1) * S]).then_inc(e1_ps, 1)
                        if slot == F_H2[c, e]:
                            if e == 0:
                                pe.wait_ge(e1_sb, 6 * i + 3 * c + 3)
                            else:
                                pe.wait_ge(e2_sb, 6 * i + 3 * c + e)
                            pe.matmul(f_bank[:, :], k("e2")[:, e * 128:(e + 1) * 128], e1t[:, e, :], start=True,
                                      stop=True).then_inc(e2_ps, 1)

            def ffn_out(i, slot, prepped):
                for t in range(8):
                    if slot == F_Y[t]:
                        if t == 0:
                            if prepped:
                                pe.wait_ge(v_sb, 4 * (i + 2) + 4)
                            else:
                                wait(pe, y_sb, 8 * i)
                        else:
                            pe.wait_ge(y_sb, 8 * i + t)
                        if t % 4 == 0:
                            pe.wait_ge(e2_sb, 6 * i + 3 * (t // 4) + 3)
                        for e in range(EP):
                            last = pe.matmul(r_bank[:, e * 128:(e + 1) * 128], e2t[:, e, t * 128:(t + 1) * 128],
                                             k("e3")[:, e * 128:(e + 1) * 128], start=True, stop=True)
                        last.then_inc(y_ps, 1)

            def body(i, par, prev, nxt):
                for slot in range(SLOTS):
                    scores(i, par, slot)
                    if slot % 4 == 0 and (slot + 4 < SLOTS or nxt):
                        if slot + 4 < SLOTS:
                            queries(i, par, slot // 4 + 1)
                        else:
                            queries(i + 1, 1 - par, 0)
                    if slot % 2 == PV_AT % 2:
                        if slot >= PV_AT:
                            pv(i, (slot - PV_AT) // 8, (SLOTS + slot - PV_AT) % 8 // 2)
                        elif prev:
                            pv(i - 1, (SLOTS + slot - PV_AT) // 8, (SLOTS + slot - PV_AT) % 8 // 2)
                    if slot % 8 == TURN_AT % 8:
                        latest = HP * i + min(slot // 4 + 2, HP + nxt)
                        if slot >= TURN_AT:
                            turn(i, (slot - TURN_AT) // 8, latest)
                        elif prev:
                            turn(i - 1, (SLOTS + slot - TURN_AT) // 8, latest)
                    if nxt:
                        prep(i + 1, 1 - par, slot)
                    if prev:
                        ffn(i - 1, 1 - par, slot)
                        ffn_out(i - 1, slot, nxt)

            pe.wait_ge(load_cst, 16)
            pe.wait_ge(load_cst2, 16)
            for n in range(HEADS):
                pe.matmul(s_bank[n // 4][:, (n % 4) * 128:(n % 4 + 1) * 128], k("wq")[:, n * 128:(n + 1) * 128],
                          k("wk"), start=True, stop=True).then_inc(qk_ps, 1)
            pe.wait_ge(wsplit, 2)
            for slot in range(P_V[1] + 1):
                prep(0, 0, slot)
            pe.wait_ge(qk_lo, 2)
            queries(0, 0, 0)
            body(0, 0, False, True)
            with pe.Fori(1, PAIRS - 1, 2) as i:
                body(i, 1, True, True)
                body(i + 1, 0, True, True)
            body(PAIRS - 1, 1, True, False)
            for slot in range(SLOTS):
                if slot < PV_AT and slot % 2 == PV_AT % 2:
                    pv(PAIRS - 1, (SLOTS + slot - PV_AT) // 8, (SLOTS + slot - PV_AT) % 8 // 2)
                if slot < TURN_AT and slot % 8 == TURN_AT % 8:
                    turn(PAIRS - 1, (SLOTS + slot - TURN_AT) // 8, HP * PAIRS)
                ffn(PAIRS - 1, 1, slot)
                ffn_out(PAIRS - 1, slot, False)

        @block.scalar
        def _(act):
            def exps(i, c):
                act.wait_ge(maxed, SLOTS * i + c + 1)
                wait(act, pvd, 4 * (HH * i + c // 8 - 2) + c % 4 + 1)
                nc.scalar.activation(p[:, c % 16, :], s_bank[c % 4][:, :], ACT.Exp, bias=nmax[:, c % 16:c % 16 + 1],
                                     accum_out=z[:, c // 8 % 2, c % 8:c % 8 + 1]).then_inc(expd, 1)

            def queries_high(i, n):
                act.wait_ge(gps, HP * i + n + 1)
                nc.scalar.copy(g[:, n % 2, :], g_bank[:, :]).then_inc(ghi, 1)

            def copy_mt(i, a):
                act.wait_ge(pvd, 4 * (HH * i + a) + 4)
                nc.scalar.copy(mt[:, :], m_bank[:, :]).then_inc(mtd, 1)

            def copy_m(i, par, a):
                act.wait_ge(turned_ps, HH * i + a + 1)
                nc.scalar.copy(m[:, par, a // 4, :, 2 * (a % 4):2 * (a % 4) + 2, :].rearrange("q j n c -> q j (n c)"),
                               g_bank[:, :].rearrange("q (j c) -> q j c", j=4)).then_inc(mevd, 1)

            def head_pairs(i, par, slot, inner, prev):
                if slot % 8 == MT_AT % 8:
                    if slot >= MT_AT:
                        if inner:
                            copy_mt(i, (slot - MT_AT) // 8)
                    elif prev:
                        copy_mt(i - 1, (SLOTS + slot - MT_AT) // 8)
                if slot % 8 == TURN_AT % 8:
                    if slot >= TURN_AT:
                        if inner:
                            copy_m(i, par, (slot - TURN_AT) // 8)
                    elif prev:
                        copy_m(i - 1, 1 - par, (SLOTS + slot - TURN_AT) // 8)

            def prep(kk, par, slot):
                for c in range(2):
                    if slot == P_H1[c]:
                        act.wait_ge(h1_ps, 2 * kk + c + 1)
                        nc.scalar.activation(h1t[:, c * S:(c + 1) * S], r_bank[:, :], ACT.Relu).then_inc(h1_sb, 1)
                    if slot == P_T[c]:
                        act.wait_ge(t_ps, 2 * kk + c + 1)
                        for b2 in range(2):
                            nc.scalar.copy(keys(kh, par, b2, c), turned(b2)).then_inc(kh_sb, 1)
                    if slot == P_V[c]:
                        act.wait_ge(v_ps, 2 * kk + c + 1)
                        src = r_bank[:, :].rearrange("q (a b d) -> q a b d", b=2, d=C)
                        nc.scalar.copy(v[0:64, par, c, :, :], src[0:64, :, 0, :]).then_inc(v_sb, 1)
                        nc.scalar.copy(v[64:128, par, c, :, :], src[64:128, :, 1, :]).then_inc(v_sb, 1)

            def ffn(i, slot):
                for c in range(2):
                    if slot == F_T[c]:
                        act.wait_ge(x2t_ps, 2 * i + c + 1)
                        nc.scalar.copy(xh[:, c * S:(c + 1) * S], f_bank[:, :]).then_inc(xh_sb, 1)
                    if slot == F_R[c]:
                        act.wait_ge(rh_ps, 2 * i + c + 1)
                        nc.scalar.activation(rh[:, c * S:(c + 1) * S], f_bank[:, :], ACT.Relu,
                                             bias=k("rb1")).then_inc(rh_sb, 1)
                    for e in range(EP):
                        if slot == F_H1[c, e]:
                            act.wait_ge(e1_ps, 6 * i + 3 * c + e + 1)
                            nc.scalar.activation(e1t[:, e, :], f_bank[:, :], ACT.Relu,
                                                 bias=k("e1b")[:, e:e + 1]).then_inc(e1_sb, 1)
                if slot == F_GATE:
                    act.wait_ge(gate, GATE * i + 2)
                    nc.scalar.activation(gt[:, 1, :, :], gt[:, 0, :, :], ACT.Exp).then_inc(gate_act, 1)
                if slot == F_GATE + 5:
                    act.wait_ge(gate, GATE * i + 16)
                    nc.scalar.activation(gs[:, 7, :], gs[:, 6, :], ACT.Exp).then_inc(gate_act, 1)

            def body(i, par, prev, nxt):
                for slot in range(SLOTS):
                    exps(i, slot)
                    if slot % 4 == 0:
                        if slot + 4 < SLOTS:
                            queries_high(i, slot // 4 + 1)
                        elif nxt:
                            queries_high(i + 1, 0)
                    head_pairs(i, par, slot, True, prev)
                    if nxt:
                        prep(i + 1, 1 - par, slot)
                    if prev:
                        ffn(i - 1, slot)

            def keys(t, par, b2, c):
                return t[:, par, b2, :].rearrange("q (d hh) -> q d hh", d=8)[:, :, 32 * c:32 * c + 32].rearrange(
                    "q d (h e) -> q d h e", h=4)

            def turned(b2):
                return r_bank[:, :].rearrange("q (h b e d) -> q b d h e", h=4, b=2, e=8)[:, b2, :, :, :]

            act.wait_ge(angle, 9)
            nc.scalar.activation(turns[:, :], ang[:, :], ACT.Sin).then_inc(sine, 1)
            for q in range(2):
                act.wait_ge(qk_ps, 4 * q + 4)
                nc.scalar.activation(qk[:, 4 * q:4 * q + 4, :], s_bank[q][:, :].rearrange("q (n c) -> q n c", n=4),
                                     ACT.Copy, scale=SCORE_SCALE).then_inc(qk_hi, 1)
            for slot in range(P_V[1] + 2):
                prep(0, 0, slot)
            queries_high(0, 0)
            body(0, 0, False, True)
            with act.Fori(1, PAIRS - 1, 2) as i:
                body(i, 1, True, True)
                body(i + 1, 0, True, True)
            body(PAIRS - 1, 1, True, False)
            for slot in range(SLOTS):
                head_pairs(PAIRS, 0, slot, False, True)
                ffn(PAIRS - 1, slot)

        @block.vector
        def _(dve):
            def maxima(i, c):
                dve.wait_ge(score, SLOTS * i + c + 1)
                nc.vector.tensor_reduce(nmax[:, c % 16:c % 16 + 1], s_bank[c % 4][:, :], AX.X, ALU.max,
                                        negate=True).then_inc(maxed, 1)

            def queries_low(i, n):
                dve.wait_ge(ghi, HP * i + n + 1)
                nc.vector.tensor_tensor(g[64:128, n % 2, :], g_bank[64:128, :], g[64:128, n % 2, :].bitcast(F32),
                                        ALU.subtract).then_inc(glo, 1)

            def recip_sums(i, a):
                dve.wait_ge(expd, SLOTS * i + 8 * a + 8)
                nc.vector.reciprocal(rz[:, a % 2, :], z[:, a % 2, :]).then_inc(rzd, 1)

            def mean(n, i, x):
                nc.vector.tensor_reduce(st[n][:, 0, :], x, AX.X, ALU.add).then_inc(ln_dve[n], 1)
                dve.wait_ge(ln_dve[n], LN_DVE * i + 1)
                nc.vector.tensor_scalar(st[n][:, 1, :], st[n][:, 0, :], -1.0 / C, None,
                                        ALU.mult).then_inc(ln_dve[n], 1)

            def rstd(n, i):
                dve.wait_ge(ln_pool[n], LN_POOL[n] * i + 2)
                nc.vector.tensor_reduce(st[n][:, 2, :], sq[n][:, :, :], AX.X, ALU.add).then_inc(ln_dve[n], 1)
                dve.wait_ge(ln_dve[n], LN_DVE * i + 3)
                nc.vector.tensor_scalar(st[n][:, 3, :], st[n][:, 2, :], 1.0 / C, LN_EPS, ALU.mult,
                                        ALU.add).then_inc(ln_dve[n], 1)

            def keys(t, par, b2, c):
                return t[:, par, b2, :].rearrange("q (d hh) -> q d hh", d=8)[:, :, 32 * c:32 * c + 32].rearrange(
                    "q d (h e) -> q d h e", h=4)

            def turned(b2):
                return r_bank[:, :].rearrange("q (h b e d) -> q b d h e", h=4, b=2, e=8)[:, b2, :, :, :]

            def prep(kk, par, slot):
                for c in range(2):
                    if slot == P_TOK[c]:
                        dve.wait_ge(tok_ps, 2 * kk + c + 1)
                        nc.vector.tensor_copy(tok[:, 4 * c:4 * c + 4, :],
                                              r_bank[:, :].rearrange("q (t c) -> q t c", t=4)).then_inc(tok_sb, 1)
                    if slot == P_T[c]:
                        for b2 in range(2):
                            dve.wait_ge(kh_sb, 4 * kk + 2 * c + 2)
                            nc.vector.tensor_tensor(keys(kl, par, b2, c), turned(b2),
                                                    keys(kh, par, b2, c).bitcast(F32),
                                                    ALU.subtract).then_inc(kl_sb, 1)
                if slot == P_LNA:
                    dve.wait_ge(tok_sb, 2 * kk + 2)
                    mean(0, kk, tok[:, :, 0:C])
                if slot == P_LNA2:
                    rstd(0, kk)
                if slot == P_LNB:
                    dve.wait_ge(ln_pool[0], 6 * kk + 6)
                    nc.vector.scalar_tensor_tensor(out=h[:, par, :, :], in0=tok[:, :, C:], scalar=0.1,
                                                   in1=xc[0][:, :, :], op0=ALU.mult, op1=ALU.add).then_inc(h_sb, 1)
                    dve.wait_ge(h_sb, kk + 1)
                    mean(1, kk, h[:, par, :, :])
                if slot == P_LNB2:
                    rstd(1, kk)

            def bcast(x):
                return x.unsqueeze(2).to_broadcast([128, 8, NE])

            def gating(i, part):
                base = GATE * i

                def done(n, ins):
                    ins.then_inc(gate, 1)

                def after(n):
                    dve.wait_ge(gate, base + n)

                rank = k("rank").unsqueeze(1).to_broadcast([128, 8, NE])
                logits = f_bank[:, 0:8 * NE].rearrange("q (t e) -> q t e", t=8)
                G, V = (lambda n: gt[:, n, :, :]), (lambda n: gs[:, n, :])
                tt, red = nc.vector.tensor_tensor, nc.vector.tensor_reduce
                if part == 0:
                    dve.wait_ge(l_ps, i + 1)
                    done(1, red(V(0), logits, AX.X, ALU.max))
                    after(1)
                    done(2, tt(G(0), logits, bcast(V(0)), ALU.subtract))
                if part == 1:
                    dve.wait_ge(gate_act, 2 * i + 1)
                    done(3, red(V(1), G(1), AX.X, ALU.add))
                    after(3)
                    done(4, nc.vector.reciprocal(V(2), V(1)))
                    after(4)
                    done(5, tt(G(2), G(1), bcast(V(2)), ALU.mult))
                if part == 2:
                    after(5)
                    done(6, red(V(3), G(2), AX.X, ALU.max))
                    after(6)
                    done(7, tt(G(3), G(2), bcast(V(3)), ALU.is_equal))
                    after(7)
                    done(8, tt(G(3), G(3), rank, ALU.mult))
                if part == 3:
                    after(8)
                    done(9, red(V(4), G(3), AX.X, ALU.max))
                    after(9)
                    done(10, tt(G(4), G(3), bcast(V(4)), ALU.is_equal))
                    after(10)
                    done(11, nc.vector.scalar_tensor_tensor(out=G(5), in0=G(4), scalar=-2.0, in1=G(2), op0=ALU.mult,
                                                            op1=ALU.add))
                if part == 4:
                    after(11)
                    done(12, red(V(5), G(5), AX.X, ALU.max))
                    after(12)
                    done(13, tt(G(6), G(5), bcast(V(5)), ALU.is_equal))
                    after(13)
                    done(14, tt(G(6), G(6), rank, ALU.mult))
                    after(14)
                    done(15, red(V(8), G(6), AX.X, ALU.max))
                    done(16, tt(V(6), V(5), V(3), ALU.subtract))
                if part == 5:
                    after(15)
                    done(17, tt(G(7), G(6), bcast(V(8)), ALU.is_equal))
                    dve.wait_ge(gate_act, 2 * i + 2)
                    done(18, nc.vector.tensor_scalar(V(9), V(7), 1.0, None, ALU.add))
                    after(18)
                    done(19, nc.vector.reciprocal(V(0), V(9)))
                    after(19)
                    done(20, tt(V(1), V(7), V(0), ALU.mult))
                if part == 6:
                    after(20)
                    tt(G(0), G(4), bcast(V(0)), ALU.mult).then_inc(gate, 1)
                    tt(G(1), G(7), bcast(V(1)), ALU.mult).then_inc(gate, 1)
                    after(22)
                    tt(G(8), G(0), G(1), ALU.add).then_inc(gated, 1)

            def ffn(i, par, slot):
                if slot == F_LN:
                    dve.wait_ge(fin_ps, i + 1)
                    nc.vector.tensor_tensor(hatt[:, :, :], h[:, par, :, :],
                                            f_bank[:, :].rearrange("q (t c) -> q t c", t=8),
                                            ALU.add).then_inc(hatt_sb, 1)
                    dve.wait_ge(hatt_sb, i + 1)
                    mean(2, i, hatt[:, :, :])
                if slot == F_LN2:
                    rstd(2, i)
                for c in range(2):
                    if slot == F_T[c]:
                        dve.wait_ge(xh_sb, 2 * i + c + 1)
                        nc.vector.tensor_tensor(xl[:, c * S:(c + 1) * S], f_bank[:, :],
                                                xh[:, c * S:(c + 1) * S].bitcast(F32),
                                                ALU.subtract).then_inc(xl_sb, 1)
                    for e in range(EP):
                        if slot == F_H2[c, e]:
                            dve.wait_ge(e2_ps, 6 * i + 3 * c + e + 1)
                            nc.vector.tensor_scalar(e2t[:, e, c * S:(c + 1) * S], f_bank[:, :],
                                                    k("e2b")[:, e:e + 1], 0.0, ALU.add, ALU.max).then_inc(e2_sb, 1)
                if slot == F_L + 1:
                    gating(i, 0)
                for part in range(1, 7):
                    if slot == F_GATE + part + (part > 4):
                        gating(i, part)
                for t in range(8):
                    if slot == F_Y[t]:
                        dve.wait_ge(y_ps, 8 * i + t + 1)
                        if t >= 2:
                            dve.wait_ge(y_pool, 40 * i + 5 * t - 5)
                        nc.vector.tensor_tensor(y[:, t % 2, :, :].rearrange("q e c -> q (e c)"), r_bank[:, 0:NE * C],
                                                k("e3b"), ALU.add).then_inc(y_sb, 1)

            def body(i, par, prev, nxt):
                for slot in range(SLOTS):
                    maxima(i, slot)
                    if slot % 4 == 1:
                        if slot + 4 < SLOTS:
                            queries_low(i, slot // 4 + 1)
                        elif nxt:
                            queries_low(i + 1, 0)
                    if slot % 8 == 1:
                        if slot >= 8:
                            recip_sums(i, slot // 8 - 1)
                        elif prev:
                            recip_sums(i - 1, HH - 1)
                    if nxt:
                        prep(i + 1, 1 - par, slot)
                    if prev:
                        ffn(i - 1, 1 - par, slot)

            def four(n):
                return cst[:, LAYOUT["fourier"][0] + n:LAYOUT["fourier"][0] + n + 1]
            period, harm, phase, quarter, shift, amp, one = (four(n) for n in range(7))
            two_pi = float(np.float32(2.0 * math.pi))
            c1 = 6.28125
            c2 = float(np.float32(int((2 * math.pi - c1) * 2 ** 21)) / 2 ** 21)
            c3 = float(np.float32(2 * math.pi - c1 - c2))
            magic = 1.5 * 2 ** 23
            pi = 3.1415925
            dve.wait_ge(load_ids, 16)
            dve.wait_ge(load_cst, 16)
            A, T = ang[:, :], turns[:, :]
            ts, stt = nc.vector.tensor_scalar, nc.vector.scalar_tensor_tensor
            nc.vector.memset(feat[:, :], 0.0).then_inc(feat_zero, 1)
            nc.vector.reciprocal(per_turn[:, :], period).then_inc(inverse, 1)
            dve.wait_ge(inverse, 1)
            ts(A, ids_sb[:, :], two_pi, per_turn[:, 0:1], ALU.mult, ALU.mult).then_inc(angle, 1)
            dve.wait_ge(angle, 1)
            ts(A, A, harm, phase, ALU.mult, ALU.add).then_inc(angle, 1)
            dve.wait_ge(angle, 2)
            ts(T, A, 1.0 / (2.0 * math.pi), quarter, ALU.mult, ALU.add).then_inc(angle, 1)
            dve.wait_ge(angle, 3)
            ts(T, T, magic, magic, ALU.add, ALU.subtract).then_inc(angle, 1)
            for n, cn in enumerate((c1, c2, c3)):
                dve.wait_ge(angle, 4 + n)
                stt(out=A, in0=T, scalar=-cn, in1=A, op0=ALU.mult, op1=ALU.add).then_inc(angle, 1)
            dve.wait_ge(angle, 7)
            ts(A, A, shift, pi, ALU.add, ALU.min).then_inc(angle, 1)
            dve.wait_ge(angle, 8)
            ts(A, A, -pi, None, ALU.max).then_inc(angle, 1)
            nc.vector.tensor_copy(wsp[:, :], cst[:, 0:SPLIT]).then_inc(wsplit, 1)
            dve.wait_ge(wsplit, 1)
            nc.vector.tensor_tensor(wsp[64:128, :], cst[64:128, 0:SPLIT], wsp[64:128, :].bitcast(F32),
                                    ALU.subtract).then_inc(wsplit, 1)
            dve.wait_ge(sine, 1)
            ts(A, T, amp, one, ALU.mult, ALU.add).then_inc(feats, 1)
            for q in range(2):
                dve.wait_ge(qk_hi, q + 1)
                stt(out=qk[64:128, 4 * q:4 * q + 4, :].rearrange("q n c -> q (n c)"), in0=s_bank[q][64:128, :],
                    scalar=SCORE_SCALE, in1=qk[64:128, 4 * q:4 * q + 4, :].rearrange("q n c -> q (n c)").bitcast(F32),
                    op0=ALU.mult, op1=ALU.subtract).then_inc(qk_lo, 1)
            for slot in range(P_V[1] + 2):
                prep(0, 0, slot)
            queries_low(0, 0)
            body(0, 0, False, True)
            with dve.Fori(1, PAIRS - 1, 2) as i:
                body(i, 1, True, True)
                body(i + 1, 0, True, True)
            body(PAIRS - 1, 1, True, False)
            for slot in range(SLOTS):
                if slot == 1:
                    recip_sums(PAIRS - 1, HH - 1)
                ffn(PAIRS - 1, 1, slot)

        @block.gpsimd
        def _(pool):
            def over_sums(i, a):
                pool.wait_ge(rzd, HH * i + a + 1)
                for hh in range(2):
                    nc.gpsimd.tensor_tensor(woz[:, a % 2, 4 * hh:4 * hh + 4, :],
                                            k("wo").rearrange("q (m c) -> q m c", m=4),
                                            rz[:, a % 2, 4 * hh:4 * hh + 4].unsqueeze(2).to_broadcast([128, 4, C]),
                                            ALU.mult).then_inc(wozd, 1)

            def wide(x):
                return x.unsqueeze(2).to_broadcast([128, 8, C])

            def centre(n, i, x):
                pool.wait_ge(ln_dve[n], LN_DVE * i + 2)
                nc.gpsimd.tensor_tensor(xc[n][:, :, :], x, wide(st[n][:, 1, :]), ALU.add).then_inc(ln_pool[n], 1)
                pool.wait_ge(ln_pool[n], LN_POOL[n] * i + 1)
                nc.gpsimd.tensor_tensor(sq[n][:, :, :], xc[n][:, :, :], xc[n][:, :, :],
                                        ALU.mult).then_inc(ln_pool[n], 1)

            def normalise(n, i, *dsts):
                pool.wait_ge(ln_dve[n], LN_DVE * i + 4)
                nc.gpsimd.tensor_tensor(st[n][:, 4, :], st[n][:, 3, :], power[:, :], ALU.pow).then_inc(ln_pool[n], 1)
                pool.wait_ge(ln_pool[n], LN_POOL[n] * i + 3)
                for dst in dsts:
                    nc.gpsimd.tensor_tensor(dst, xc[n][:, :, :], wide(st[n][:, 4, :]),
                                            ALU.mult).then_inc(ln_pool[n], 1)

            def prep(kk, par, slot):
                if slot == P_LNA:
                    centre(0, kk, tok[:, :, 0:C])
                if slot == P_LNA2:
                    normalise(0, kk, xc[0][:, :, :])
                    pool.wait_ge(ln_pool[0], 6 * kk + 4)
                    for n, (w, op) in enumerate((("gamma", ALU.mult), ("beta", ALU.add))):
                        nc.gpsimd.tensor_tensor(xc[0][:, :, :], xc[0][:, :, :],
                                                k(w).unsqueeze(1).to_broadcast([128, 8, C]), op).then_inc(ln_pool[0], 1)
                        if n == 0:
                            pool.wait_ge(ln_pool[0], 6 * kk + 5)
                if slot == P_LNB:
                    centre(1, kk, h[:, par, :, :])
                if slot == P_LNB2:
                    normalise(1, kk, xn[:, :, 0, :], xn[:, :, 1, :])

            def ffn(i, slot):
                if slot == F_LN:
                    centre(2, i, hatt[:, :, :])
                if slot == F_LN2:
                    normalise(2, i, x2[:, :, 0, :], x2[:, :, 1, :])
                for t in range(8):
                    if slot == F_Y[t]:
                        base = 40 * i + 5 * t
                        if t == 0:
                            pool.wait_ge(gated, i + 1)
                            pool.wait_ge(stored, 16 * GROUPS + 32 * i)
                        pool.wait_ge(y_sb, 8 * i + t + 1)
                        yt, s2 = y[:, t % 2, :, :], ys[:, t % 2, :, :]
                        tt = nc.gpsimd.tensor_tensor
                        tt(yt, yt, gt[:, 8, t, :].unsqueeze(2).to_broadcast([128, NE, C]),
                           ALU.mult).then_inc(y_pool, 1)
                        pool.wait_ge(y_pool, base + 1)
                        tt(s2[:, 0:3, :], yt[:, 0:3, :], yt[:, 3:6, :], ALU.add).then_inc(y_pool, 1)
                        pool.wait_ge(y_pool, base + 2)
                        tt(s2[:, 3, :], s2[:, 0, :], s2[:, 1, :], ALU.add).then_inc(y_pool, 1)
                        tt(s2[:, 2, :], s2[:, 2, :], hatt[:, t, :], ALU.add).then_inc(y_pool, 1)
                        pool.wait_ge(y_pool, base + 4)
                        tt(o[:, t, :], s2[:, 2, :], s2[:, 3, :], ALU.add).then_inc(y_pool, 1)

            def body(i, par, prev, nxt):
                for slot in range(SLOTS):
                    if slot % 8 == 1:
                        if slot >= 8:
                            over_sums(i, slot // 8 - 1)
                        elif prev:
                            over_sums(i - 1, HH - 1)
                    if nxt:
                        prep(i + 1, 1 - par, slot)
                    if prev:
                        ffn(i - 1, slot)

            nc.gpsimd.memset(power[:, :], -0.5).then_inc(power_set, 1)
            pool.wait_ge(power_set, 1)
            pool.wait_ge(load_cst2, 16)
            for slot in range(P_V[1] + 2):
                prep(0, 0, slot)
            body(0, 0, False, True)
            with pool.Fori(1, PAIRS - 1, 2) as i:
                body(i, 1, True, True)
                body(i + 1, 0, True, True)
            body(PAIRS - 1, 1, True, False)
            for slot in range(SLOTS):
                if slot == 1:
                    over_sums(PAIRS - 1, HH - 1)
                ffn(PAIRS - 1, slot)


def laid_out(x):
    w = {n[3:]: np.asarray(a) for n, a in x.items() if n.startswith("L0_")}

    def rows(a):
        a = np.asarray(a, np.float32)
        a = a.reshape(a.shape[0], -1)
        return np.concatenate([a, np.zeros((128 - a.shape[0], a.shape[1]), np.float32)], 0)

    def every_row(a):
        return np.repeat(a.reshape(1, -1), 128, 0)

    def diagonal(a):
        d = np.zeros((EP, 2, a.shape[1], 2, a.shape[2]), np.float32)
        for e in range(2):
            d[:, e, :, e, :] = a[e::2]
        return d.transpose(1, 2, 0, 3, 4).reshape(2 * a.shape[1], -1)

    def cols(a):
        return a.reshape(EP, 2 * C).T

    parts = {}
    parts["wv"] = np.tile(w["attn_Wv"].T, (2, 2))
    r1 = np.tile(w["ffn_router_w1"], (2, 1))
    parts["rw1"] = np.concatenate([r1, np.zeros((128, 128 - r1.shape[1]), np.float32)], 1)
    parts["e1"] = np.tile(w["ffn_expert_w1"].transpose(1, 0, 2).reshape(C, -1), (2, 1))
    wq = w["attn_Wq"].reshape(HEADS, KD, C).transpose(1, 0, 2)
    parts["wq"] = rows(np.concatenate([wq, wq], 2))
    parts["wk"] = rows(np.tile(w["attn_Wk"], (1, 2)))
    wo = w["attn_Wo"].T.reshape(C, 8, C).transpose(1, 0, 2).reshape(4, 128, C)
    parts["wo"] = wo.transpose(1, 0, 2).reshape(128, -1)
    parts["w1"] = rows(np.concatenate([w["tok_W1"], w["tok_b1"].reshape(1, -1)], 0))
    zero = np.zeros((FD, C), np.float32)
    parts["wres"] = rows(np.concatenate([
        np.concatenate([zero, w["tok_b2"].reshape(1, -1)], 0),
        np.concatenate([w["tok_Wres"], w["tok_bres"].reshape(1, -1)], 0)], 1))
    parts["w2"] = w["tok_W2"]
    parts["gamma"], parts["beta"] = every_row(w["tok_gamma"]), every_row(w["tok_beta"])
    one = np.ones(1, np.float32)
    parts["rw2"] = rows(np.concatenate([w["ffn_router_w2"], w["ffn_router_b2"].reshape(1, -1)], 0))
    parts["rb1"] = rows(np.concatenate([w["ffn_router_b1"], one]).reshape(-1, 1))
    parts["e1b"], parts["e2b"] = cols(w["ffn_expert_b1"]), cols(w["ffn_expert_b2"])
    parts["e2"], parts["e3"] = diagonal(w["ffn_expert_w2"]), diagonal(w["ffn_expert_w3"])
    parts["e3b"] = every_row(w["ffn_expert_b3"])
    parts["ident"] = np.eye(128, dtype=np.float32)
    parts["rank"] = every_row(np.arange(NE, 0, -1, dtype=np.float32))

    n = len(PERIODS)
    f = np.zeros((32, 7), np.float32)
    f[:, 0] = 1.0
    f[:FD, 0] = np.repeat(np.array(PERIODS, np.float32), 2 * HARM)
    f[:FD, 1] = np.tile(np.repeat(np.arange(1, HARM + 1, dtype=np.float32), 2), n)
    f[:FD, 2] = np.repeat(w["tok_ph"].reshape(-1), 2)
    f[:FD, 3] = np.tile(np.array([0.0, 0.25], np.float32), n * HARM)
    f[:FD, 4] = np.tile(np.array([0.0, math.pi / 2], np.float32), n * HARM)
    f[:FD, 5] = np.repeat(w["tok_hw"].reshape(-1), 2)
    f[FD, 6] = 1.0
    parts["fourier"] = np.tile(f, (GROUPS, 1))

    consts = np.zeros((128, WIDTH), np.float32)
    for name, (a, b) in LAYOUT.items():
        consts[:, a:b] = parts[name]

    t = np.stack([np.asarray(x[name]) for name in ("x", "itok_BS_0_23", "itok_BS_0_11", "itok_BS_0_30")])
    t = t.reshape(n, GROUPS, 2, 2, HEADS, KD).transpose(1, 0, 2, 4, 3, 5).reshape(GROUPS, n, GCOL)
    ids = np.zeros((GROUPS, 32, GCOL), t.dtype)
    ids[:, :FD] = np.repeat(t, 2 * HARM, 1)
    return ids.reshape(128, GCOL), consts


def kernel(**inputs):
    import concourse.bacc as bacc
    from concourse.bass_utils import run_bass_kernel_spmd

    ids, consts = laid_out(inputs)
    nc = bacc.Bacc("TRN2", target_bir_lowering=False, num_devices=1)
    ids_d = nc.dram_tensor("ids", ids.shape, mybir.dt.from_np(ids.dtype), kind="ExternalInput").ap()
    cst_d = nc.dram_tensor("consts", consts.shape, mybir.dt.float32, kind="ExternalInput").ap()
    out_d = nc.dram_tensor("tower_out", (B, S, C), mybir.dt.float32, kind="ExternalOutput").ap()
    tower(nc, ids_d, cst_d, out_d)
    r = run_bass_kernel_spmd(nc, [{"ids": ids, "consts": consts}], core_ids=[0])
    return r.results[0]["tower_out"]
```

```python
import math
from contextlib import ExitStack

import numpy as np
from concourse import mybir

B, S, C = 16, 512, 64
HEADS, KD = 8, 64
NE = 6
EP = NE // 2
HARM, PERIODS = 3, (7.0, 24.0, 12.0, 1.0)
FD = 2 * HARM * len(PERIODS)
FR = FD + 1
PAIRS = B // 2
TOK = 2 * S
HP = 2 * HEADS
HH = HP // 2
SLOTS = 4 * HP
QUARTERS = 4
QT = TOK // QUARTERS
GCOL = PAIRS * QT
LN_EPS = 1e-5
SCORE_SCALE = float(np.float32(1.0) / np.sqrt(KD // HEADS).astype(np.float32))

LAYOUT, WIDTH = {}, 0
for _name, _w in (("fourier", 7), ("w1", QUARTERS * 128), ("wres", QUARTERS * 128), ("w2", C),
                  ("wq", HEADS * 128), ("wk", 128), ("wv", 128), ("rw1", 2 * 128), ("e1", EP * 128),
                  ("gamma", C), ("beta", C), ("wo", 4 * C), ("rw2", 2 * NE), ("rb1", 1), ("e1b", EP),
                  ("e2", EP * 128), ("e2b", EP),
                  ("e3", EP * 128), ("e3b", NE * C), ("ident", 128), ("rank", NE)):
    LAYOUT[_name] = (WIDTH, WIDTH + _w)
    WIDTH += _w
SPLIT = slice(LAYOUT["wv"][0], LAYOUT["e1"][1])
CUTS = (0, LAYOUT["w1"][0], LAYOUT["wq"][0], LAYOUT["wv"][0], WIDTH)

Q_AT, Q_ACT, Q_DVE = 0, 0, 1
WARM0, WARM, WARM_FIN, WARM_T = 12, 12, 8, 20
FOUR_AT, FOUR_SINE, FOUR_WEIGH = (2, 8, 14, 20, 26, 32, 38, 44, 50), 56, 56
RZ_AT, PV_AT, MT_AT, TURN_AT, M_ACT = 8, (13, 14, 16, 17), 17, 19, 18
P = {
    "H1": (4, 5), "H1_ACT": (3, 5), "TOK": (10, 10, 12, 12), "TOK_DVE": (9, 12),
    "LNA": 12, "SQA": 12, "LNA2": 13, "LNB": 20, "SQB": 20, "LNB2": 22,
    "T": (26, 29), "T_ACT": (25, 28), "T_DVE": (28, 31), "V": (32, 33), "V_ACT": (32, 33),
}
F = {
    "FIN": (12, 13, 14, 15), "LN": 15, "SQ": 17, "LN2": 17,
    "T": (22, 24), "T_ACT": (20, 23), "T_DVE": (22, 24), "R": 25, "R_ACT": 26,
    "L": (31, 31), "GATE": (31, 33, 34, 35, 36, 38, 38), "GATE_ACT": (30, 37),
    "H1": (35, 36, 38, 39, 42, 44), "H1_ACT": (33, 36, 38, 39, 41, 43),
    "H2": (37, 39, 41, 43, 45, 47), "H2_DVE": (38, 40, 41, 42, 44, 52),
    "Y": (45, 48, 49, 52, 56, 58, 60, 62), "Y_DVE": (45, 48, 50, 53, 56, 58, 60, 62),
}
L = {
    "FIN": (12, 13, 13, 15), "LN": 10, "SQ": 14, "LN2": 13,
    "T": (18, 24), "T_ACT": (16, 22), "T_DVE": (14, 20), "R": 26, "R_ACT": 32,
    "L": (28, 29), "GATE": (33, 37, 39, 41, 42, 45, 47), "GATE_ACT": (35, 43),
    "H1": (36, 36, 39, 41, 44, 46), "H1_ACT": (37, 37, 40, 43, 47, 50),
    "H2": (40, 43, 44, 46, 48, 53), "H2_DVE": (42, 44, 46, 47, 48, 54),
    "Y": (46, 48, 50, 53, 55, 57, 58, 59), "Y_DVE": (47, 50, 53, 57, 59, 60, 60, 62),
}


def at(slot, offset, i):
    a = (slot - offset) // 8
    if (slot - offset) % 8:
        return None
    return (i, a) if a >= 0 else (i - 1, HH + a)


def tower(nc, ids, consts, out):
    F32, F32R, I32 = mybir.dt.float32, mybir.dt.float32r, mybir.dt.int32
    ALU, ACT, AX = mybir.AluOpType, mybir.ActivationFunctionType, mybir.AxisListType

    ctx = ExitStack()
    with ctx:
        def sb(name, shape, dt=F32):
            return ctx.enter_context(nc.sbuf_tensor(name, shape, dt))

        def pb(name):
            return ctx.enter_context(nc.psum_tensor(name, [128, 512], F32))

        def sem(name):
            return ctx.enter_context(nc.semaphore(name))

        cst = sb("cst", [128, WIDTH])

        def k(name):
            return cst[:, LAYOUT[name][0]:LAYOUT[name][1]]

        wsp = sb("wsp", [128, SPLIT.stop - SPLIT.start], F32R)
        qk = sb("qk", [128, HEADS, 128], F32R)
        per_turn = sb("per_turn", [128, 1])
        power = sb("power", [128, 8])
        spare = sb("spare", [128, 128])
        feat = sb("feat", [128, PAIRS, QT])
        feat_now = sb("feat_now", [128, QT])
        h1t = sb("h1t", [128, TOK])
        tok = sb("tok", [128, 8, 128])
        xc = [sb(f"xc{n}", [128, 8, C]) for n in range(3)]
        sq = [sb(f"sq{n}", [128, 8, C]) for n in range(2)]
        sq = [sq[0], sq[0], sq[1]]
        st = [sb(f"st{n}", [128, 5, 8]) for n in range(3)]
        h = sb("h", [128, 2, 8, C])
        xn = sb("xn", [128, 8, 2, C])
        kh = sb("kh", [128, 2, 2, S], F32R)
        kl = sb("kl", [128, 2, 2, S], F32R)
        v = sb("v", [128, 2, 2, 4, C])
        g = sb("g", [128, 2, S], F32R)
        p = sb("p", [128, 16, S])
        nmax = sb("nmax", [128, 16])
        z = sb("z", [128, 2, 8])
        rz = sb("rz", [128, 2, 8])
        woz = sb("woz", [128, 2, 8, C])
        mt = sb("mt", [128, S])
        m = sb("m", [128, 2, 2, 4, HEADS, C])
        flat = m[:, :, :, :, :, :].rearrange("q a b j n c -> q (a b j n c)")
        turns, ids_sb = (flat[:, n * GCOL:(n + 1) * GCOL] for n in (2, 3))
        ids_sb = ids_sb.bitcast(I32)
        flat_feat = feat[:, :, :].rearrange("q p t -> q (p t)")
        four_cols = (slice(0, QT), slice(QT, 2 * QT), slice(2 * QT, GCOL))
        hatt = sb("hatt", [128, 8, C])
        x2 = sb("x2", [128, 8, 2, C])
        xh = sb("xh", [128, TOK], F32R)
        xl = sb("xl", [128, TOK], F32R)
        rh = sb("rh", [128, S])
        gt = sb("gt", [128, 9, 8, NE])
        gs = sb("gs", [128, 10, 8])
        e1t = sb("e1t", [128, EP, S])
        e2t = sb("e2t", [128, EP, TOK])
        y = sb("y", [128, 2, NE, C])
        ys = sb("ys", [128, 2, 4, C])
        o = sb("o", [128, 8, C])

        s_bank = [pb(f"s_bank{n}") for n in range(4)]
        m_bank, g_bank, r_bank, f_bank = pb("m_bank"), pb("g_bank"), pb("r_bank"), pb("f_bank")
        shared = {"T": (f_bank,), "R": f_bank, "L": f_bank, "H1": (r_bank,), "H2": (f_bank,), "Y": (r_bank,)}
        alone = {"T": (f_bank, s_bank[0]), "R": s_bank[1], "L": m_bank, "H1": (r_bank, s_bank[3]),
                                "H2": (f_bank, s_bank[0]), "Y": (g_bank, m_bank, s_bank[1], s_bank[2])}

        load_ids = [sem(f"load_ids{n}") for n in range(2)]
        load_four, load_qk, load_tok, load_rest = [
            sem(x) for x in ("load_four", "load_qk", "load_tok", "load_rest")]
        feat_in, stored = sem("feat_in"), sem("stored")
        (inverse, power_set, spare_set, angle, sine, feats, wsplit, qk_ps, qk_hi, qk_lo) = [
            sem(x) for x in ("inverse", "power_set", "spare_set", "angle", "sine", "feats", "wsplit", "qk_ps", "qk_hi", "qk_lo")]
        (score, maxed, expd, rzd, wozd, pvd, mtd, turned_ps, mevd, gps, ghi, glo) = [
            sem(x) for x in ("score", "maxed", "expd", "rzd", "wozd", "pvd", "mtd", "turned_ps", "mevd", "gps", "ghi", "glo")]
        (h1_ps, h1_sb, tok_ps, tok_sb, h_sb, t_ps, kh_sb, kl_sb, v_ps, v_sb) = [
            sem(x) for x in ("h1_ps", "h1_sb", "tok_ps", "tok_sb", "h_sb", "t_ps", "kh_sb", "kl_sb", "v_ps", "v_sb")]
        ln_dve = [sem(f"ln_dve{n}") for n in range(3)]
        ln_step = [sem(f"ln_step{n}") for n in range(3)]
        ln_sq = [sem(f"ln_sq{n}") for n in range(3)]
        (fin_ps, hatt_sb, x2t_ps, xh_sb, xl_sb, rh_ps, rh_sb, l_ps, gate, gate_act) = [
            sem(x) for x in ("fin_ps", "hatt_sb", "x2t_ps", "xh_sb", "xl_sb", "rh_ps", "rh_sb", "l_ps", "gate", "gate_act")]
        (e1_ps, e1_sb, e2_ps, e2_sb, y_ps, y_sb, y_pool, y_dve, gated) = [
            sem(x) for x in ("e1_ps", "e1_sb", "e2_ps", "e2_sb", "y_ps", "y_sb", "y_pool", "y_dve", "gated")]

        LN_DVE, LN_STEP = 4, 4
        GATE = 22

        def wait(eng, s, value):
            if isinstance(value, int) and value <= 0:
                return
            eng.wait_ge(s, value)

        def weighted_sum(eng, ops, t, done, base):
            yt, s2 = y[:, t % 2, :, :], ys[:, t % 2, :, :]
            ops.tensor_tensor(yt, yt, gt[:, 8, t, :].unsqueeze(2).to_broadcast([128, NE, C]),
                              ALU.mult).then_inc(done, 1)
            eng.wait_ge(done, base + 1)
            ops.tensor_tensor(s2[:, 0:3, :], yt[:, 0:3, :], yt[:, 3:6, :], ALU.add).then_inc(done, 1)
            eng.wait_ge(done, base + 2)
            ops.tensor_tensor(s2[:, 3, :], s2[:, 0, :], s2[:, 1, :], ALU.add).then_inc(done, 1)
            ops.tensor_tensor(s2[:, 2, :], s2[:, 2, :], hatt[:, t, :], ALU.add).then_inc(done, 1)
            eng.wait_ge(done, base + 4)
            ops.tensor_tensor(o[:, t, :], s2[:, 2, :], s2[:, 3, :], ALU.add).then_inc(done, 1)

        def four(n):
            return cst[:, LAYOUT["fourier"][0] + n:LAYOUT["fourier"][0] + n + 1]
        period, harm, phase, quarter, shift, amp, one = (four(n) for n in range(7))
        two_pi = float(np.float32(2.0 * math.pi))
        c1 = 6.28125
        c2 = float(np.float32(int((2 * math.pi - c1) * 2 ** 21)) / 2 ** 21)
        c3 = float(np.float32(2 * math.pi - c1 - c2))
        magic = 1.5 * 2 ** 23
        pi = 3.1415925

        def reduced(eng, ops, n, step):
            ts, stt = ops.tensor_scalar, ops.scalar_tensor_tensor
            A, T = flat_feat[:, four_cols[n]], turns[:, four_cols[n]]
            if step == 0:
                eng.wait_ge(load_ids[min(n, 1)], 16)
                ins = ts(A, ids_sb[:, four_cols[n]], two_pi, per_turn[:, 0:1], ALU.mult, ALU.mult)
            else:
                eng.wait_ge(angle, 9 * n + step)
            if step == 1:
                ins = ts(A, A, harm, phase, ALU.mult, ALU.add)
            if step == 2:
                ins = ts(T, A, 1.0 / (2.0 * math.pi), quarter, ALU.mult, ALU.add)
            if step == 3:
                ins = ts(T, T, magic, magic, ALU.add, ALU.subtract)
            if step in (4, 5, 6):
                ins = stt(out=A, in0=T, scalar=-(c1, c2, c3)[step - 4], in1=A, op0=ALU.mult, op1=ALU.add)
            if step == 7:
                ins = ts(A, A, shift, pi, ALU.add, ALU.min)
            if step == 8:
                ins = ts(A, A, -pi, None, ALU.max)
            ins.then_inc(angle, 1)

        def weigh(eng, ops, n):
            eng.wait_ge(sine, n + 1)
            ops.tensor_scalar(flat_feat[:, four_cols[n]], turns[:, four_cols[n]], amp, one, ALU.mult, ALU.add).then_inc(feats, 1)

        block = ctx.enter_context(nc.Block())

        @block.sync
        def _(sp):
            def load(n, done):
                sp.dma_start(cst[:, CUTS[n]:CUTS[n + 1]], consts[:, CUTS[n]:CUTS[n + 1]]).then_inc(done, 16)

            sp.dma_start(ids_sb[:, 0:QT], ids[:, 0:QT]).then_inc(load_ids[0], 16)
            load(0, load_four)
            load(1, load_tok)
            sp.dma_start(ids_sb[:, QT:], ids[:, QT:]).then_inc(load_ids[1], 16)
            load(2, load_qk)
            load(3, load_rest)

            def store(i, last=False):
                sp.wait_ge(y_pool, 40 * i + (20 if last else 40))
                if last:
                    sp.wait_ge(y_dve, 20)
                for b2 in range(2):
                    dst = out[2 * i + b2, :, :].rearrange("(h d) c -> d h c", d=KD)
                    sp.dma_start(dst, o[64 * b2:64 * b2 + 64, :, :]).then_inc(stored, 16)

            def fetch(kk):
                if isinstance(kk, int):
                    sp.wait_ge(feats, 3)
                sp.wait_ge(tok_ps, 2 * kk)
                sp.dma_start(feat_now[:, :], feat[:, kk, :]).then_inc(feat_in, 16)

            fetch(2)
            with sp.Fori(1, PAIRS - 2) as i:
                fetch(i + 2)
                store(i - 1)
            for n in range(PAIRS - 3, PAIRS):
                store(n, n == PAIRS - 1)
            sp.wait_ge(stored, 32 * PAIRS)

        @block.tensor
        def _(pe):
            wsl = {n: wsp[:, LAYOUT[n][0] - SPLIT.start:LAYOUT[n][1] - SPLIT.start] for n in ("wv", "rw1", "e1")}

            def both(dst, weights, high, low):
                pe.matmul(dst, weights, high, start=True, stop=False)
                return pe.matmul(dst, weights, low, start=False, stop=True)

            def scores(i, par, c):
                n, mm = c // 4, c % 4
                if mm == 0:
                    pe.wait_ge(glo, HP * i + n + 1)
                wait(pe, expd, SLOTS * i + c - 3)
                both(s_bank[mm][:, :], g[:, n % 2, mm * 128:(mm + 1) * 128],
                     kh[:, par, n // HEADS, :], kl[:, par, n // HEADS, :]).then_inc(score, 1)

            def queries(i, par, n):
                wait(pe, glo, HP * i + n)
                if n == 0:
                    wait(pe, kl_sb, 4 * i + 4)
                both(g_bank[:, :], qk[:, n % HEADS, :], kh[:, par, n // HEADS, :],
                     kl[:, par, n // HEADS, :]).then_inc(gps, 1)

            def pv(i, a, mm):
                if mm == 0:
                    pe.wait_ge(wozd, 2 * (HH * i + a) + 2)
                    wait(pe, mevd, HH * i + a)
                for hh in range(2):
                    last = pe.matmul(m_bank[64 * hh:64 * hh + 64, :], woz[:, a % 2, 4 * hh + mm, :],
                                     p[:, 8 * (a % 2) + 4 * hh + mm, :], start=(mm == 0), stop=(mm == 3))
                last.then_inc(pvd, 1)

            def turn(i, a):
                pe.wait_ge(mtd, HH * i + a + 1)
                for jj in range(4):
                    last = pe.transpose(m_bank[:, jj * 128:(jj + 1) * 128], mt[:, jj * 128:(jj + 1) * 128], k("ident"))
                last.then_inc(turned_ps, 1)

            def prep(kk, par, slot, banks=(r_bank, r_bank)):
                kk_static = isinstance(kk, int)
                two = banks[0] is not banks[1]
                features = feat[:, kk, :] if kk_static else feat_now[:, :]
                for c in range(2):
                    if slot == P["H1"][c]:
                        if c == 0:
                            if kk_static:
                                pe.wait_ge(feats, kk + 1)
                            else:
                                pe.wait_ge(feat_in, 16 * (kk - 1))
                        elif not two:
                            pe.wait_ge(h1_sb, 2 * kk + 1)
                        for half in range(2):
                            q = 2 * c + half
                            last = pe.matmul(banks[c][:, half * QT:(half + 1) * QT], k("w1")[:, q * 128:(q + 1) * 128],
                                             features, start=True, stop=True)
                        last.then_inc(h1_ps, 1)
                    for half in range(2):
                        if slot != P["TOK"][2 * c + half]:
                            continue
                        if half == 0:
                            pe.wait_ge(h1_sb, 2 * kk + (c + 1 if two else 2))
                            if c and not two:
                                pe.wait_ge(tok_sb, 2 * kk + 1)
                        for t in range(2 * half, 2 * half + 2):
                            cols = slice((4 * c + t) * 128, (4 * c + t + 1) * 128)
                            q = (4 * c + t) // 2
                            pe.matmul(banks[c][:, t * 128:(t + 1) * 128], features[:, t % 2 * 128:(t % 2 + 1) * 128],
                                      k("wres")[:, q * 128:(q + 1) * 128], start=True, stop=False,
                                      skip_group_check=True)
                            last = pe.matmul(banks[c][:, t * 128:t * 128 + C], h1t[:, cols], k("w2"), start=False,
                                             stop=True, skip_group_check=True)
                        if half:
                            last.then_inc(tok_ps, 1)
                    if slot == P["T"][c]:
                        if c == 0:
                            pe.wait_ge(ln_step[1], LN_STEP * kk + 4)
                        elif not two:
                            pe.wait_ge(kl_sb, 4 * kk + 2)
                        for t in range(4):
                            src = xn[:, 4 * c + t, :, :].rearrange("q a c -> q (a c)")
                            last = pe.transpose(banks[c][:, t * 128:(t + 1) * 128], src, k("ident"))
                        last.then_inc(t_ps, 1)
                    if slot == P["V"][c]:
                        if c == 0:
                            pe.wait_ge(kl_sb, 4 * kk + 4)
                        elif not two:
                            pe.wait_ge(v_sb, 4 * kk + 2)
                        def by_value_row(x):
                            return x[:, par, c, :].rearrange("q (a b) -> q b a", a=8)
                        both(banks[c][:, :], wsl["wv"], by_value_row(kh), by_value_row(kl)).then_inc(v_ps, 1)

            def ffn(i, par, slot, prepped, f=F, banks=shared):
                for jj in range(4):
                    if slot == f["FIN"][jj]:
                        if jj == 0:
                            pe.wait_ge(mevd, HH * i + HH)
                        for b2 in range(2):
                            last = pe.matmul(f_bank[64 * b2:64 * b2 + 64, :], v[:, par, b2, jj, :],
                                             m[:, par, b2, jj, :, :], start=(jj == 0), stop=(jj == 3))
                        if jj == 3:
                            last.then_inc(fin_ps, 1)
                for c in range(2):
                    if slot == f["T"][c]:
                        if c == 0:
                            if banks is alone:
                                pe.wait_ge(ln_dve[2], LN_DVE * i + 1)
                                warm(WARM_T, s_bank[3])
                            pe.wait_ge(ln_step[2], LN_STEP * i + 4)
                        elif banks is shared:
                            pe.wait_ge(xl_sb, 2 * i + 1)
                        for t in range(4):
                            src = x2[:, 4 * c + t, :, :].rearrange("q a c -> q (a c)")
                            last = pe.transpose(banks["T"][c % len(banks["T"])][:, t * 128:(t + 1) * 128], src, k("ident"))
                        last.then_inc(x2t_ps, 1)
                if slot == f["R"]:
                    pe.wait_ge(xl_sb, 2 * i + 2)
                    for c in range(2):
                        weights = wsl["rw1"][:, c * 128:(c + 1) * 128]
                        pe.matmul(banks["R"][:, :], weights, xh[:, c * S:(c + 1) * S], start=(c == 0), stop=False)
                        last = pe.matmul(banks["R"][:, :], weights, xl[:, c * S:(c + 1) * S], start=False, stop=(c == 1))
                    last.then_inc(rh_ps, 1)
                for half in range(2):
                    if slot != f["L"][half]:
                        continue
                    pe.wait_ge(rh_sb, i + 1)
                    for t in range(2 * half, 2 * half + 2):
                        dst = banks["L"][:, 0:8 * NE].rearrange("q (c t e) -> q c t e", c=2, t=4)[:, :, t, :]
                        last = pe.matmul(dst, rh[:, t * 128:(t + 1) * 128], k("rw2"), start=True, stop=True)
                    if half:
                        last.then_inc(l_ps, 1)
                n1, n2 = len(banks["H1"]), len(banks["H2"])
                for c in range(2):
                    for e in range(EP):
                        j = EP * c + e
                        if slot == f["H1"][j]:
                            if j >= n1:
                                pe.wait_ge(e1_sb, 6 * i + j - n1 + 1)
                            elif prepped:
                                pe.wait_ge(v_sb, 4 * (i + 2) + 4)
                            both(banks["H1"][j % n1][:, :], wsl["e1"][:, e * 128:(e + 1) * 128],
                                 xh[:, c * S:(c + 1) * S], xl[:, c * S:(c + 1) * S]).then_inc(e1_ps, 1)
                        if slot == f["H2"][j]:
                            pe.wait_ge(e1_sb, 6 * i + j + 1)
                            if j >= n2:
                                pe.wait_ge(e2_sb, 6 * i + j - n2 + 1)
                            elif j == 0:
                                pe.wait_ge(gate, GATE * i + 2)
                            pe.matmul(banks["H2"][j % n2][:, :], k("e2")[:, e * 128:(e + 1) * 128], e1t[:, e, :],
                                      start=True, stop=True).then_inc(e2_ps, 1)

            def ffn_out(i, slot, f=F, banks=shared):
                n = len(banks["Y"])
                for t in range(8):
                    if slot == f["Y"][t]:
                        if t >= n:
                            pe.wait_ge(y_sb, 8 * i + t - n + 1)
                        elif banks is shared:
                            pe.wait_ge(e1_sb, 6 * i + 6)
                        if t % 4 == 0:
                            pe.wait_ge(e2_sb, 6 * i + 3 * (t // 4) + 3)
                        for e in range(EP):
                            last = pe.matmul(banks["Y"][t % n][:, e * 128:(e + 1) * 128],
                                             e2t[:, e, t * 128:(t + 1) * 128],
                                             k("e3")[:, e * 128:(e + 1) * 128], start=True, stop=True)
                        last.then_inc(y_ps, 1)

            def products(i, slot, own, prev):
                for mm in range(4):
                    found = at(slot, PV_AT[mm], i)
                    if found and (own if slot >= PV_AT[mm] else prev):
                        pv(*found, mm)
                found = at(slot, TURN_AT, i)
                if found and (own if slot >= TURN_AT else prev):
                    turn(*found)

            def body(i, par, prev, nxt):
                for slot in range(SLOTS):
                    scores(i, par, slot)
                    if slot % 4 == Q_AT and (slot + 4 < SLOTS or nxt):
                        if slot + 4 < SLOTS:
                            queries(i, par, slot // 4 + 1)
                        else:
                            queries(i + 1, 1 - par, 0)
                    products(i, slot, True, prev)
                    if nxt:
                        prep(i + 1, 1 - par, slot)
                    if prev:
                        ffn(i - 1, 1 - par, slot, nxt)
                        ffn_out(i - 1, slot)

            def warm(count, bank):
                for _ in range(count):
                    pe.matmul(bank[:, 0:2 * C], spare[:, 0:128], spare[:, 0:128], start=True, stop=True)

            pe.wait_ge(spare_set, 1)
            warm(WARM0, m_bank)
            pe.wait_ge(load_tok, 16)
            for slot in range(SLOTS):
                if slot == P["T"][0]:
                    pe.wait_ge(load_qk, 16)
                    for n in range(HEADS):
                        pe.matmul(s_bank[n // 4][:, (n % 4) * 128:(n % 4 + 1) * 128],
                                  k("wq")[:, n * 128:(n + 1) * 128], k("wk"), start=True, stop=True).then_inc(qk_ps, 1)
                if slot == P["T"][0]:
                    pe.wait_ge(load_rest, 16)
                    pe.wait_ge(wsplit, 2)
                    pe.wait_ge(ln_dve[1], 2)
                    warm(WARM, m_bank)
                prep(0, 0, slot, (r_bank, f_bank))
            pe.wait_ge(qk_lo, 2)
            queries(0, 0, 0)
            body(0, 0, False, True)
            with pe.Fori(1, PAIRS - 1, 2) as i:
                body(i, 1, True, True)
                body(i + 1, 0, True, True)
            body(PAIRS - 1, 1, True, False)
            for slot in range(SLOTS):
                products(PAIRS, slot, False, True)
                if slot == L["FIN"][0]:
                    warm(WARM_FIN, s_bank[3])
                ffn(PAIRS - 1, 1, slot, False, L, alone)
                ffn_out(PAIRS - 1, slot, L, alone)

        @block.scalar
        def _(act):
            def exps(i, c):
                act.wait_ge(maxed, SLOTS * i + c + 1)
                wait(act, pvd, 4 * (HH * i + c // 8 - 2) + c % 4 + 1)
                nc.scalar.activation(p[:, c % 16, :], s_bank[c % 4][:, :], ACT.Exp, bias=nmax[:, c % 16:c % 16 + 1],
                                     accum_out=z[:, c // 8 % 2, c % 8:c % 8 + 1]).then_inc(expd, 1)

            def queries_high(i, n):
                act.wait_ge(gps, HP * i + n + 1)
                nc.scalar.copy(g[:, n % 2, :], g_bank[:, :]).then_inc(ghi, 1)

            def copy_m(i, par, a):
                act.wait_ge(turned_ps, HH * i + a + 1)
                nc.scalar.copy(m[:, par, a // 4, :, 2 * (a % 4):2 * (a % 4) + 2, :].rearrange("q j n c -> q j (n c)"),
                               m_bank[:, :].rearrange("q (j c) -> q j c", j=4)).then_inc(mevd, 1)

            def squares(n, i):
                act.wait_ge(ln_step[n], LN_STEP * i + 1)
                nc.scalar.activation(sq[n][:, :, :], xc[n][:, :, :], ACT.Square).then_inc(ln_sq[n], 1)

            def prep(kk, par, slot, banks=(r_bank, r_bank)):
                for n, first in ((0, P["SQA"]), (1, P["SQB"])):
                    if slot == first:
                        squares(n, kk)
                for c in range(2):
                    if slot == P["H1_ACT"][c]:
                        act.wait_ge(h1_ps, 2 * kk + c + 1)
                        nc.scalar.activation(h1t[:, c * S:(c + 1) * S], banks[c][:, :], ACT.Relu).then_inc(h1_sb, 1)
                    if slot == P["T_ACT"][c]:
                        act.wait_ge(t_ps, 2 * kk + c + 1)
                        for b2 in range(2):
                            nc.scalar.copy(keys(kh, par, b2, c), turned(banks[c], b2)).then_inc(kh_sb, 1)
                    if slot == P["V_ACT"][c]:
                        act.wait_ge(v_ps, 2 * kk + c + 1)
                        src = banks[c][:, :].rearrange("q (a b d) -> q a b d", b=2, d=C)
                        nc.scalar.copy(v[0:64, par, c, :, :], src[0:64, :, 0, :]).then_inc(v_sb, 1)
                        nc.scalar.copy(v[64:128, par, c, :, :], src[64:128, :, 1, :]).then_inc(v_sb, 1)

            def ffn(i, slot, f=F, banks=shared):
                if slot == f["SQ"]:
                    squares(2, i)
                for c in range(2):
                    if slot == f["T_ACT"][c]:
                        act.wait_ge(x2t_ps, 2 * i + c + 1)
                        nc.scalar.copy(xh[:, c * S:(c + 1) * S], banks["T"][c % len(banks["T"])][:, :]).then_inc(xh_sb, 1)
                    for e in range(EP):
                        if slot == f["H1_ACT"][EP * c + e]:
                            act.wait_ge(e1_ps, 6 * i + 3 * c + e + 1)
                            nc.scalar.activation(e1t[:, e, :], banks["H1"][(EP * c + e) % len(banks["H1"])][:, :], ACT.Relu,
                                                 bias=k("e1b")[:, e:e + 1]).then_inc(e1_sb, 1)
                if slot == f["R_ACT"]:
                    act.wait_ge(rh_ps, i + 1)
                    nc.scalar.activation(rh[:, :], banks["R"][:, :], ACT.Relu, bias=k("rb1")).then_inc(rh_sb, 1)
                if slot == f["GATE_ACT"][0]:
                    act.wait_ge(gate, GATE * i + 2)
                    nc.scalar.activation(gt[:, 1, :, :], gt[:, 0, :, :], ACT.Exp).then_inc(gate_act, 1)
                if slot == f["GATE_ACT"][1]:
                    act.wait_ge(gate, GATE * i + 16)
                    nc.scalar.activation(gs[:, 7, :], gs[:, 6, :], ACT.Exp).then_inc(gate_act, 1)

            def body(i, par, prev, nxt):
                for slot in range(SLOTS):
                    exps(i, slot)
                    if not prev and slot == FOUR_SINE:
                        sines(2)
                    if slot % 4 == Q_ACT:
                        if slot + 4 < SLOTS:
                            queries_high(i, slot // 4 + 1)
                        elif nxt:
                            queries_high(i + 1, 0)
                    found = at(slot, M_ACT, i)
                    if slot >= M_ACT and found:
                        copy_m(i, par, found[1])
                    elif prev and found:
                        copy_m(i - 1, 1 - par, found[1])
                    if nxt:
                        prep(i + 1, 1 - par, slot)
                    if prev:
                        ffn(i - 1, slot)

            def keys(t, par, b2, c):
                return t[:, par, b2, :].rearrange("q (d hh) -> q d hh", d=8)[:, :, 32 * c:32 * c + 32].rearrange(
                    "q d (h e) -> q d h e", h=4)

            def turned(bank, b2):
                return bank[:, :].rearrange("q (h b e d) -> q b d h e", h=4, b=2, e=8)[:, b2, :, :, :]

            def sines(n):
                act.wait_ge(angle, 9 * n + 9)
                nc.scalar.activation(turns[:, four_cols[n]], flat_feat[:, four_cols[n]], ACT.Sin).then_inc(sine, 1)

            sines(0)
            for slot in range(SLOTS):
                prep(0, 0, slot, (r_bank, f_bank))
                if slot == P["H1_ACT"][1]:
                    sines(1)
                if slot == P["SQA"]:
                    for q in range(2):
                        act.wait_ge(qk_ps, 4 * q + 4)
                        nc.scalar.activation(qk[:, 4 * q:4 * q + 4, :], s_bank[q][:, :].rearrange("q (n c) -> q n c", n=4),
                                             ACT.Copy, scale=SCORE_SCALE).then_inc(qk_hi, 1)
            queries_high(0, 0)
            body(0, 0, False, True)
            with act.Fori(1, PAIRS - 1, 2) as i:
                body(i, 1, True, True)
                body(i + 1, 0, True, True)
            body(PAIRS - 1, 1, True, False)
            for slot in range(SLOTS):
                found = at(slot, M_ACT, PAIRS)
                if slot < M_ACT and found:
                    copy_m(PAIRS - 1, 1, found[1])
                ffn(PAIRS - 1, slot, L, alone)

        @block.vector
        def _(dve):
            def maxima(i, c):
                dve.wait_ge(score, SLOTS * i + c + 1)
                nc.vector.tensor_reduce(nmax[:, c % 16:c % 16 + 1], s_bank[c % 4][:, :], AX.X, ALU.max,
                                        negate=True).then_inc(maxed, 1)

            def queries_low(i, n):
                dve.wait_ge(ghi, HP * i + n + 1)
                nc.vector.tensor_tensor(g[64:128, n % 2, :], g_bank[64:128, :], g[64:128, n % 2, :].bitcast(F32),
                                        ALU.subtract).then_inc(glo, 1)

            def recip_sums(i, a):
                dve.wait_ge(expd, SLOTS * i + 8 * a + 8)
                nc.vector.reciprocal(rz[:, a % 2, :], z[:, a % 2, :]).then_inc(rzd, 1)

            def copy_mt(i, a):
                dve.wait_ge(pvd, 4 * (HH * i + a) + 4)
                nc.vector.tensor_copy(mt[:, :], m_bank[:, :]).then_inc(mtd, 1)

            def mean(n, i, x):
                nc.vector.tensor_reduce(st[n][:, 0, :], x, AX.X, ALU.add).then_inc(ln_dve[n], 1)
                dve.wait_ge(ln_dve[n], LN_DVE * i + 1)
                nc.vector.tensor_scalar(st[n][:, 1, :], st[n][:, 0, :], -1.0 / C, None,
                                        ALU.mult).then_inc(ln_dve[n], 1)

            def rstd(n, i):
                dve.wait_ge(ln_sq[n], i + 1)
                nc.vector.tensor_reduce(st[n][:, 2, :], sq[n][:, :, :], AX.X, ALU.add).then_inc(ln_dve[n], 1)
                dve.wait_ge(ln_dve[n], LN_DVE * i + 3)
                nc.vector.tensor_scalar(st[n][:, 3, :], st[n][:, 2, :], 1.0 / C, LN_EPS, ALU.mult,
                                        ALU.add).then_inc(ln_dve[n], 1)

            def keys(t, par, b2, c):
                return t[:, par, b2, :].rearrange("q (d hh) -> q d hh", d=8)[:, :, 32 * c:32 * c + 32].rearrange(
                    "q d (h e) -> q d h e", h=4)

            def turned(bank, b2):
                return bank[:, :].rearrange("q (h b e d) -> q b d h e", h=4, b=2, e=8)[:, b2, :, :, :]

            def wide(x):
                return x.unsqueeze(2).to_broadcast([128, 8, C])

            def centred(n, x, i=0):
                dve.wait_ge(ln_dve[n], LN_DVE * i + 2)
                nc.vector.tensor_tensor(xc[n][:, :, :], x, wide(st[n][:, 1, :]), ALU.add).then_inc(ln_step[n], 1)

            def scaled(n, dst, i=0):
                dve.wait_ge(ln_step[n], LN_STEP * i + 2)
                nc.vector.tensor_tensor(dst, xc[n][:, :, :], wide(st[n][:, 4, :]), ALU.mult).then_inc(ln_step[n], 1)

            def prep(kk, par, slot, banks=(r_bank, r_bank)):
                first = banks[0] is not banks[1]
                for c in range(2):
                    if slot == P["TOK_DVE"][c]:
                        dve.wait_ge(tok_ps, 2 * kk + c + 1)
                        nc.vector.tensor_copy(tok[:, 4 * c:4 * c + 4, :],
                                              banks[c][:, :].rearrange("q (t c) -> q t c", t=4)).then_inc(tok_sb, 1)
                    if slot == P["T_DVE"][c]:
                        for b2 in range(2):
                            dve.wait_ge(kh_sb, 4 * kk + 2 * c + 2)
                            nc.vector.tensor_tensor(keys(kl, par, b2, c), turned(banks[c], b2),
                                                    keys(kh, par, b2, c).bitcast(F32),
                                                    ALU.subtract).then_inc(kl_sb, 1)
                if slot == P["LNA"]:
                    dve.wait_ge(tok_sb, 2 * kk + 2)
                    mean(0, kk, tok[:, :, 0:C])
                    if first:
                        centred(0, tok[:, :, 0:C])
                if slot == P["LNA2"]:
                    rstd(0, kk)
                    if first:
                        scaled(0, xc[0][:, :, :])
                        dve.wait_ge(ln_step[0], 3)
                        nc.vector.tensor_tensor(xc[0][:, :, :], xc[0][:, :, :],
                                                k("gamma").unsqueeze(1).to_broadcast([128, 8, C]),
                                                ALU.mult).then_inc(ln_step[0], 1)
                if slot == P["LNB"]:
                    dve.wait_ge(ln_step[0], LN_STEP * kk + 4)
                    nc.vector.tensor_tensor(xc[0][:, :, :], xc[0][:, :, :],
                                            k("beta").unsqueeze(1).to_broadcast([128, 8, C]),
                                            ALU.add).then_inc(h_sb, 1)
                    dve.wait_ge(h_sb, 2 * kk + 1)
                    nc.vector.scalar_tensor_tensor(out=h[:, par, :, :], in0=tok[:, :, C:], scalar=0.1,
                                                   in1=xc[0][:, :, :], op0=ALU.mult, op1=ALU.add).then_inc(h_sb, 1)
                    dve.wait_ge(h_sb, 2 * kk + 2)
                    mean(1, kk, h[:, par, :, :])
                    if first:
                        centred(1, h[:, par, :, :])
                if slot == P["LNB2"]:
                    rstd(1, kk)
                    if first:
                        scaled(1, xn[:, :, 0, :])

            def bcast(x):
                return x.unsqueeze(2).to_broadcast([128, 8, NE])

            def gating(i, part, bank):
                base = GATE * i

                def done(n, ins):
                    ins.then_inc(gate, 1)

                def after(n):
                    dve.wait_ge(gate, base + n)

                rank = k("rank").unsqueeze(1).to_broadcast([128, 8, NE])
                logits = bank[:, 0:8 * NE].rearrange("q (t e) -> q t e", t=8)
                G, V = (lambda n: gt[:, n, :, :]), (lambda n: gs[:, n, :])
                tt, red = nc.vector.tensor_tensor, nc.vector.tensor_reduce
                if part == 0:
                    dve.wait_ge(l_ps, i + 1)
                    done(1, red(V(0), logits, AX.X, ALU.max))
                    after(1)
                    done(2, tt(G(0), logits, bcast(V(0)), ALU.subtract))
                if part == 1:
                    dve.wait_ge(gate_act, 2 * i + 1)
                    done(3, red(V(1), G(1), AX.X, ALU.add))
                    after(3)
                    done(4, nc.vector.reciprocal(V(2), V(1)))
                    after(4)
                    done(5, tt(G(2), G(1), bcast(V(2)), ALU.mult))
                if part == 2:
                    after(5)
                    done(6, red(V(3), G(2), AX.X, ALU.max))
                    after(6)
                    done(7, tt(G(3), G(2), bcast(V(3)), ALU.is_equal))
                    after(7)
                    done(8, tt(G(3), G(3), rank, ALU.mult))
                if part == 3:
                    after(8)
                    done(9, red(V(4), G(3), AX.X, ALU.max))
                    after(9)
                    done(10, tt(G(4), G(3), bcast(V(4)), ALU.is_equal))
                    after(10)
                    done(11, nc.vector.scalar_tensor_tensor(out=G(5), in0=G(4), scalar=-2.0, in1=G(2), op0=ALU.mult,
                                                            op1=ALU.add))
                if part == 4:
                    after(11)
                    done(12, red(V(5), G(5), AX.X, ALU.max))
                    after(12)
                    done(13, tt(G(6), G(5), bcast(V(5)), ALU.is_equal))
                    after(13)
                    done(14, tt(G(6), G(6), rank, ALU.mult))
                    after(14)
                    done(15, red(V(8), G(6), AX.X, ALU.max))
                    done(16, tt(V(6), V(5), V(3), ALU.subtract))
                if part == 5:
                    after(15)
                    done(17, tt(G(7), G(6), bcast(V(8)), ALU.is_equal))
                    dve.wait_ge(gate_act, 2 * i + 2)
                    done(18, nc.vector.tensor_scalar(V(9), V(7), 1.0, None, ALU.add))
                    after(18)
                    done(19, nc.vector.reciprocal(V(0), V(9)))
                    after(19)
                    done(20, tt(V(1), V(7), V(0), ALU.mult))
                if part == 6:
                    after(20)
                    tt(G(0), G(4), bcast(V(0)), ALU.mult).then_inc(gate, 1)
                    tt(G(1), G(7), bcast(V(1)), ALU.mult).then_inc(gate, 1)
                    after(22)
                    tt(G(8), G(0), G(1), ALU.add).then_inc(gated, 1)

            def ffn(i, par, slot, f=F, banks=shared):
                if slot == f["LN"]:
                    dve.wait_ge(fin_ps, i + 1)
                    nc.vector.tensor_tensor(hatt[:, :, :], h[:, par, :, :],
                                            f_bank[:, :].rearrange("q (t c) -> q t c", t=8),
                                            ALU.add).then_inc(hatt_sb, 1)
                    dve.wait_ge(hatt_sb, i + 1)
                    mean(2, i, hatt[:, :, :])
                    if banks is alone:
                        centred(2, hatt[:, :, :], i)
                if slot == f["LN2"]:
                    rstd(2, i)
                    if banks is alone:
                        scaled(2, x2[:, :, 0, :], i)
                for c in range(2):
                    if slot == f["T_DVE"][c]:
                        dve.wait_ge(xh_sb, 2 * i + c + 1)
                        nc.vector.tensor_tensor(xl[:, c * S:(c + 1) * S], banks["T"][c % len(banks["T"])][:, :],
                                                xh[:, c * S:(c + 1) * S].bitcast(F32),
                                                ALU.subtract).then_inc(xl_sb, 1)
                    for e in range(EP):
                        if slot == f["H2_DVE"][EP * c + e]:
                            dve.wait_ge(e2_ps, 6 * i + 3 * c + e + 1)
                            nc.vector.tensor_scalar(e2t[:, e, c * S:(c + 1) * S], banks["H2"][(EP * c + e) % len(banks["H2"])][:, :],
                                                    k("e2b")[:, e:e + 1], 0.0, ALU.add, ALU.max).then_inc(e2_sb, 1)
                for part in range(7):
                    if slot == f["GATE"][part]:
                        gating(i, part, banks["L"])
                for t in range(8):
                    if slot == f["Y_DVE"][t]:
                        dve.wait_ge(y_ps, 8 * i + t + 1)
                        if banks is shared and t >= 2:
                            dve.wait_ge(y_pool, 40 * i + 5 * t - 5)
                        elif t >= 2 and t % 2 == 0:
                            dve.wait_ge(y_pool, 40 * i + 5 * (t // 2))
                        nc.vector.tensor_tensor(y[:, t % 2, :, :].rearrange("q e c -> q (e c)"),
                                                banks["Y"][t % len(banks["Y"])][:, 0:NE * C],
                                                k("e3b"), ALU.add).then_inc(y_sb, 1)
                        if banks is alone and t % 2:
                            dve.wait_ge(y_sb, 8 * i + t + 1)
                            dve.wait_ge(gated, i + 1)
                            dve.wait_ge(stored, 32 * i)
                            weighted_sum(dve, nc.vector, t, y_dve, 5 * (t // 2))

            def body(i, par, prev, nxt):
                for slot in range(SLOTS):
                    maxima(i, slot)
                    if not prev and slot in FOUR_AT:
                        reduced(dve, nc.vector, 2, FOUR_AT.index(slot))
                    if slot % 4 == Q_DVE:
                        if slot + 4 < SLOTS:
                            queries_low(i, slot // 4 + 1)
                        elif nxt:
                            queries_low(i + 1, 0)
                    found = at(slot, MT_AT, i)
                    if found and (slot >= MT_AT or prev):
                        copy_mt(*found)
                    found = at(slot, RZ_AT, i)
                    if found and (slot >= RZ_AT or prev):
                        recip_sums(*found)
                    if nxt:
                        prep(i + 1, 1 - par, slot)
                    if prev:
                        ffn(i - 1, 1 - par, slot)

            dve.wait_ge(load_four, 16)
            nc.vector.reciprocal(per_turn[:, :], period).then_inc(inverse, 1)
            dve.wait_ge(inverse, 1)
            for step in range(9):
                reduced(dve, nc.vector, 0, step)
            weigh(dve, nc.vector, 0)
            for step in range(9):
                reduced(dve, nc.vector, 1, step)
            weigh(dve, nc.vector, 1)
            for slot in range(SLOTS):
                prep(0, 0, slot, (r_bank, f_bank))
                if slot == P["LNA"]:
                    dve.wait_ge(load_qk, 16)
                    dve.wait_ge(load_rest, 16)
                    nc.vector.tensor_copy(wsp[:, :], cst[:, SPLIT]).then_inc(wsplit, 1)
                if slot == P["LNA2"]:
                    dve.wait_ge(wsplit, 1)
                    nc.vector.tensor_tensor(wsp[64:128, :], cst[64:128, SPLIT], wsp[64:128, :].bitcast(F32),
                                            ALU.subtract).then_inc(wsplit, 1)
                if slot == P["LNB2"]:
                    for q in range(2):
                        dve.wait_ge(qk_hi, q + 1)
                        nc.vector.scalar_tensor_tensor(
                            out=qk[64:128, 4 * q:4 * q + 4, :].rearrange("q n c -> q (n c)"), in0=s_bank[q][64:128, :],
                            scalar=SCORE_SCALE,
                            in1=qk[64:128, 4 * q:4 * q + 4, :].rearrange("q n c -> q (n c)").bitcast(F32),
                            op0=ALU.mult, op1=ALU.subtract).then_inc(qk_lo, 1)
            queries_low(0, 0)
            body(0, 0, False, True)
            with dve.Fori(1, PAIRS - 1, 2) as i:
                body(i, 1, True, True)
                body(i + 1, 0, True, True)
            body(PAIRS - 1, 1, True, False)
            for slot in range(SLOTS):
                found = at(slot, RZ_AT, PAIRS)
                if slot < RZ_AT and found:
                    recip_sums(*found)
                found = at(slot, MT_AT, PAIRS)
                if slot < MT_AT and found:
                    copy_mt(*found)
                ffn(PAIRS - 1, 1, slot, L, alone)

        @block.gpsimd
        def _(pool):
            def over_sums(i, a):
                pool.wait_ge(rzd, HH * i + a + 1)
                for hh in range(2):
                    nc.gpsimd.tensor_tensor(woz[:, a % 2, 4 * hh:4 * hh + 4, :],
                                            k("wo").rearrange("q (m c) -> q m c", m=4),
                                            rz[:, a % 2, 4 * hh:4 * hh + 4].unsqueeze(2).to_broadcast([128, 4, C]),
                                            ALU.mult).then_inc(wozd, 1)

            def wide(x):
                return x.unsqueeze(2).to_broadcast([128, 8, C])

            def centre(n, i, x):
                pool.wait_ge(ln_dve[n], LN_DVE * i + 2)
                nc.gpsimd.tensor_tensor(xc[n][:, :, :], x, wide(st[n][:, 1, :]), ALU.add).then_inc(ln_step[n], 1)

            def normalise(n, i, *dsts):
                pool.wait_ge(ln_dve[n], LN_DVE * i + 4)
                nc.gpsimd.tensor_tensor(st[n][:, 4, :], st[n][:, 3, :], power[:, :], ALU.pow).then_inc(ln_step[n], 1)
                pool.wait_ge(ln_step[n], LN_STEP * i + 2)
                for dst in dsts:
                    nc.gpsimd.tensor_tensor(dst, xc[n][:, :, :], wide(st[n][:, 4, :]),
                                            ALU.mult).then_inc(ln_step[n], 1)

            def deviation(n, i, dst):
                pool.wait_ge(ln_dve[n], LN_DVE * i + 4)
                nc.gpsimd.tensor_tensor(st[n][:, 4, :], st[n][:, 3, :], power[:, :], ALU.pow).then_inc(ln_step[n], 1)
                if dst is not None:
                    pool.wait_ge(ln_step[n], LN_STEP * i + 2)
                    nc.gpsimd.tensor_tensor(dst, xc[n][:, :, :], wide(st[n][:, 4, :]), ALU.mult).then_inc(ln_step[n], 1)

            def prep(kk, par, slot):
                if slot == P["LNA"]:
                    centre(0, kk, tok[:, :, 0:C])
                if slot == P["LNA2"]:
                    normalise(0, kk, xc[0][:, :, :])
                    pool.wait_ge(ln_step[0], LN_STEP * kk + 3)
                    nc.gpsimd.tensor_tensor(xc[0][:, :, :], xc[0][:, :, :],
                                            k("gamma").unsqueeze(1).to_broadcast([128, 8, C]),
                                            ALU.mult).then_inc(ln_step[0], 1)
                if slot == P["LNB"]:
                    centre(1, kk, h[:, par, :, :])
                if slot == P["LNB2"]:
                    normalise(1, kk, xn[:, :, 0, :], xn[:, :, 1, :])

            def ffn(i, slot, f=F, last=False):
                if slot == f["LN"] and not last:
                    centre(2, i, hatt[:, :, :])
                if slot == f["LN2"] and last:
                    deviation(2, i, x2[:, :, 1, :])
                elif slot == f["LN2"]:
                    normalise(2, i, x2[:, :, 0, :], x2[:, :, 1, :])
                for t in range(8):
                    if slot == f["Y_DVE"][t] and not (last and t % 2):
                        if t == 0:
                            pool.wait_ge(gated, i + 1)
                            wait(pool, stored, 32 * i)
                        pool.wait_ge(y_sb, 8 * i + t + 1)
                        weighted_sum(pool, nc.gpsimd, t, y_pool, 40 * i + 5 * (t // 2 if last else t))

            def body(i, par, prev, nxt):
                for slot in range(SLOTS):
                    if not prev and slot == FOUR_WEIGH:
                        weigh(pool, nc.gpsimd, 2)
                    found = at(slot, RZ_AT, i)
                    if found and (slot >= RZ_AT or prev):
                        over_sums(*found)
                    if nxt:
                        prep(i + 1, 1 - par, slot)
                    if prev:
                        ffn(i - 1, slot)

            nc.gpsimd.memset(spare[:, :], 0.0).then_inc(spare_set, 1)
            nc.gpsimd.memset(power[:, :], -0.5).then_inc(power_set, 1)
            pool.wait_ge(power_set, 1)
            deviation(0, 0, None)
            deviation(1, 0, xn[:, :, 1, :])
            pool.wait_ge(load_rest, 16)
            body(0, 0, False, True)
            with pool.Fori(1, PAIRS - 1, 2) as i:
                body(i, 1, True, True)
                body(i + 1, 0, True, True)
            body(PAIRS - 1, 1, True, False)
            for slot in range(SLOTS):
                found = at(slot, RZ_AT, PAIRS)
                if slot < RZ_AT and found:
                    over_sums(*found)
                ffn(PAIRS - 1, slot, L, True)


def laid_out(x):
    w = {n[3:]: np.asarray(a) for n, a in x.items() if n.startswith("L0_")}

    def rows(a):
        a = np.asarray(a, np.float32)
        a = a.reshape(a.shape[0], -1)
        return np.concatenate([a, np.zeros((128 - a.shape[0], a.shape[1]), np.float32)], 0)

    def every_row(a):
        return np.repeat(a.reshape(1, -1), 128, 0)

    def diagonal(a):
        d = np.zeros((EP, 2, a.shape[1], 2, a.shape[2]), np.float32)
        for e in range(2):
            d[:, e, :, e, :] = a[e::2]
        return d.transpose(1, 2, 0, 3, 4).reshape(2 * a.shape[1], -1)

    def cols(a):
        return a.reshape(EP, 2 * C).T

    parts = {}
    parts["wv"] = np.tile(w["attn_Wv"].T, (2, 2))
    r1 = w["ffn_router_w1"]
    parts["rw1"] = np.zeros((2, C, 2, 2, C), np.float32)
    for half in range(2):
        parts["rw1"][:, :, half, half, :r1.shape[1]] = r1
    parts["rw1"] = parts["rw1"].reshape(128, -1)
    parts["e1"] = np.tile(w["ffn_expert_w1"].transpose(1, 0, 2).reshape(C, -1), (2, 1))
    wq = w["attn_Wq"].reshape(HEADS, KD, C).transpose(1, 0, 2)
    parts["wq"] = rows(np.concatenate([wq, wq], 2))
    parts["wk"] = rows(np.tile(w["attn_Wk"], (1, 2)))
    wo = w["attn_Wo"].T.reshape(C, 8, C).transpose(1, 0, 2).reshape(4, 128, C)
    parts["wo"] = wo.transpose(1, 0, 2).reshape(128, -1)
    def in_quarters(a):
        d = np.zeros((QUARTERS, 32, QUARTERS, a.shape[1]), np.float32)
        for q in range(QUARTERS):
            d[q, :FR, q, :] = a
        return d.reshape(128, -1)

    parts["w1"] = in_quarters(np.concatenate([w["tok_W1"], w["tok_b1"].reshape(1, -1)], 0))
    zero = np.zeros((FD, C), np.float32)
    parts["wres"] = in_quarters(np.concatenate([
        np.concatenate([zero, w["tok_b2"].reshape(1, -1)], 0),
        np.concatenate([w["tok_Wres"], w["tok_bres"].reshape(1, -1)], 0)], 1))
    parts["w2"] = w["tok_W2"]
    parts["gamma"], parts["beta"] = every_row(w["tok_gamma"]), every_row(w["tok_beta"])
    one = np.ones(1, np.float32)
    r2 = np.concatenate([w["ffn_router_w2"], w["ffn_router_b2"].reshape(1, -1)], 0)
    parts["rw2"] = np.zeros((2, C, 2, NE), np.float32)
    for half in range(2):
        parts["rw2"][half, :len(r2), half] = r2
    parts["rw2"] = parts["rw2"].reshape(128, -1)
    b1 = np.concatenate([w["ffn_router_b1"], one])
    parts["rb1"] = np.tile(np.concatenate([b1, np.zeros(C - len(b1), np.float32)]), 2).reshape(-1, 1)
    parts["e1b"], parts["e2b"] = cols(w["ffn_expert_b1"]), cols(w["ffn_expert_b2"])
    parts["e2"], parts["e3"] = diagonal(w["ffn_expert_w2"]), diagonal(w["ffn_expert_w3"])
    parts["e3b"] = every_row(w["ffn_expert_b3"])
    parts["ident"] = np.eye(128, dtype=np.float32)
    parts["rank"] = every_row(np.arange(NE, 0, -1, dtype=np.float32))

    n = len(PERIODS)
    f = np.zeros((32, 7), np.float32)
    f[:, 0] = 1.0
    f[:FD, 0] = np.repeat(np.array(PERIODS, np.float32), 2 * HARM)
    f[:FD, 1] = np.tile(np.repeat(np.arange(1, HARM + 1, dtype=np.float32), 2), n)
    f[:FD, 2] = np.repeat(w["tok_ph"].reshape(-1), 2)
    f[:FD, 3] = np.tile(np.array([0.0, 0.25], np.float32), n * HARM)
    f[:FD, 4] = np.tile(np.array([0.0, math.pi / 2], np.float32), n * HARM)
    f[:FD, 5] = np.repeat(w["tok_hw"].reshape(-1), 2)
    f[FD, 6] = 1.0
    parts["fourier"] = np.tile(f, (QUARTERS, 1))

    consts = np.zeros((128, WIDTH), np.float32)
    for name, (a, b) in LAYOUT.items():
        consts[:, a:b] = parts[name]

    t = np.stack([np.asarray(x[name]) for name in ("x", "itok_BS_0_23", "itok_BS_0_11", "itok_BS_0_30")])
    t = t.reshape(n, PAIRS, 2, HEADS, KD).transpose(0, 1, 3, 2, 4).reshape(n, PAIRS, QUARTERS, QT).transpose(2, 0, 1, 3)
    ids = np.zeros((QUARTERS, 32, PAIRS, QT), t.dtype)
    ids[:, :FD] = np.repeat(t, 2 * HARM, 1)
    return ids.reshape(128, GCOL), consts


def kernel(**inputs):
    import concourse.bacc as bacc
    from concourse.bass_utils import run_bass_kernel_spmd

    ids, consts = laid_out(inputs)
    nc = bacc.Bacc("TRN2", target_bir_lowering=False, num_devices=1)
    ids_d = nc.dram_tensor("ids", ids.shape, mybir.dt.from_np(ids.dtype), kind="ExternalInput").ap()
    cst_d = nc.dram_tensor("consts", consts.shape, mybir.dt.float32, kind="ExternalInput").ap()
    out_d = nc.dram_tensor("tower_out", (B, S, C), mybir.dt.float32, kind="ExternalOutput").ap()
    tower(nc, ids_d, cst_d, out_d)
    r = run_bass_kernel_spmd(nc, [{"ids": ids, "consts": consts}], core_ids=[0])
    return r.results[0]["tower_out"]
```
